# Optimizing a Trainium2 kernel written in Bass

```python
import numpy as np
import jax
import jax.numpy as jnp

def _softmax(x, axis=-1):
    return jax.nn.softmax(x, axis=axis)

def _gelu(x):
    return jax.nn.gelu(x, approximate=True)

def _silu(x):
    return jax.nn.silu(x)

def _sigmoid(x):
    return jax.nn.sigmoid(x)

def _layernorm(x, axis=-1, eps=1e-05):
    m = jnp.mean(x, axis=axis, keepdims=True)
    v = jnp.var(x, axis=axis, keepdims=True)
    return (x - m) / jnp.sqrt(v + eps)

def _scatter_add(tgt, idx, src, axis=0):
    return tgt.at[idx].add(src)

def _segment_sum(src, seg, n):
    return jax.ops.segment_sum(src, seg, n)
kernel_name = 'mk_adaln_ffn_d1_seqx_r4_e0216b'

def setup_inputs(seed: int=0):
    np.random.seed(seed)
    _w = jnp.asarray

    def _rec_inputs():
        import jax
        import jax.numpy as jnp
        _rk = jax.random.key(seed)
        x = -7.109e-05 + 0.9999 * jax.random.normal(jax.random.fold_in(_rk, 1), (64, 64, 512), jnp.float32)
        _lenS = 64 - jax.random.randint(jax.random.fold_in(_rk, 7), (64,), 0, max(1, 64 // 4) + 1, jnp.int32)
        _lenS2 = 64 - jax.random.randint(jax.random.fold_in(_rk, 8), (64,), 0, max(1, 64 // 4) + 1, jnp.int32)
        itok_B_1_198 = jax.random.randint(jax.random.fold_in(_rk, 11), (64,), 1, 199, jnp.int32)
        return (x, itok_B_1_198)
    x, itok_B_1_198 = _rec_inputs()

    def _L0_cond_setup():
        import jax, jax.numpy as jnp
        import numpy as np
        B, C, T = (128, 64, 512)
        S, D = (200, 64)
        key = jax.random.key(seed)
        k1, k2, k3 = jax.random.split(key, 3)
        x = jax.random.normal(k1, (B, C, T), dtype=jnp.float32)
        conditions = jax.random.randint(k2, (B,), 0, S, dtype=jnp.int64)
        weights = jax.random.normal(k3, (S, C, D), dtype=jnp.float32) / jnp.sqrt(jnp.float32(C))
        return {'x': x, 'conditions': conditions, 'weights': weights}
    _L0_cond_all = _L0_cond_setup()
    _L0_cond_in = {k: v for k, v in _L0_cond_all.items() if k in ('weights',)}
    del _L0_cond_all

    def _L0_ffn_setup():
        import jax, jax.numpy as jnp
        import numpy as np
        B, T, D = (1, 256, 512)
        F_DIM = 352
        E = 8
        TOPK = 2
        key = jax.random.key(seed)
        ks = jax.random.split(key, 5)
        x = jax.random.normal(ks[0], (B, T, D), dtype=jnp.float32)
        gate_w = jax.random.normal(ks[1], (E, D), dtype=jnp.float32) * 0.02
        gate_proj = jax.random.normal(ks[2], (E, F_DIM, D), dtype=jnp.float32) * 0.02
        up_proj = jax.random.normal(ks[3], (E, F_DIM, D), dtype=jnp.float32) * 0.02
        down_proj = jax.random.normal(ks[4], (E, D, F_DIM), dtype=jnp.float32) * 0.02
        return {'x': x, 'gate_w': gate_w, 'gate_proj': gate_proj, 'up_proj': up_proj, 'down_proj': down_proj}
    _L0_ffn_all = _L0_ffn_setup()
    _L0_ffn_in = {k: v for k, v in _L0_ffn_all.items() if k in ('gate_w', 'gate_proj', 'up_proj', 'down_proj')}
    del _L0_ffn_all
    return {'x': x, 'itok_B_1_198': itok_B_1_198, 'L0_cond_weights': _L0_cond_in['weights'], 'L0_ffn_gate_w': _L0_ffn_in['gate_w'], 'L0_ffn_gate_proj': _L0_ffn_in['gate_proj'], 'L0_ffn_up_proj': _L0_ffn_in['up_proj'], 'L0_ffn_down_proj': _L0_ffn_in['down_proj']}

def reference(x, itok_B_1_198, L0_cond_weights, L0_ffn_gate_w, L0_ffn_gate_proj, L0_ffn_up_proj, L0_ffn_down_proj):
    import jax
    import jax.numpy as jnp

    def _L0_cond_ref(x, conditions, weights):
        import jax, jax.numpy as jnp
        import numpy as np
        B, C, T = (128, 64, 512)
        S, D = (200, 64)
        w = weights[conditions]
        return jnp.einsum('bct,bcd->bdt', x, w)

    def _L0_ffn_ref(x, gate_w, gate_proj, up_proj, down_proj):
        import jax, jax.numpy as jnp
        import numpy as np
        B, T, D = (1, 256, 512)
        F_DIM = 352
        E = 8
        TOPK = 2
        b, t, d = x.shape
        x_flat = x.reshape(-1, d)
        n = x_flat.shape[0]
        router_logits = x_flat @ gate_w.T
        top_w, sel = jax.lax.top_k(router_logits, TOPK)
        top_w = jax.nn.softmax(top_w, axis=-1)
        tok_ids = jnp.arange(n)[:, None]
        tw = jnp.zeros((n, E), dtype=x.dtype).at[tok_ids, sel].add(top_w)
        g = jnp.einsum('nd,efd->enf', x_flat, gate_proj)
        u = jnp.einsum('nd,efd->enf', x_flat, up_proj)
        h = jax.nn.silu(g) * u
        eo = jnp.einsum('enf,edf->end', h, down_proj)
        out = jnp.einsum('end,ne->nd', eo, tw)
        return out.reshape(b, t, d)
    x = x + _L0_ffn_ref(_L0_cond_ref(x, itok_B_1_198, L0_cond_weights), L0_ffn_gate_w, L0_ffn_gate_proj, L0_ffn_up_proj, L0_ffn_down_proj)
    return x

_drawn_inputs = setup_inputs


def setup_inputs(seed=0):
    import zlib

    import numpy as np

    out = dict(_drawn_inputs(seed))
    spreads = {}
    factors = {}
    for name, (base, spread) in spreads.items():
        noise = np.random.default_rng([zlib.crc32(name.encode()), seed]).standard_normal(out[name].shape)
        drawn = base * np.exp(spread * noise) if base else spread * noise
        out[name] = jnp.asarray(drawn.astype(out[name].dtype))
    for name, factor in factors.items():
        out[name] = (out[name] * factor).astype(out[name].dtype)
    return out
```

```python
from contextlib import ExitStack

import concourse.bass as bass
from concourse import mybir

P = 128
ALU = mybir.AluOpType
ACT = mybir.ActivationFunctionType
AX = mybir.AxisListType
F32 = mybir.dt.float32
BF16 = mybir.dt.bfloat16
I32 = mybir.dt.int32

TOPK = 2
GROUP = 4
XSLOTS = 4
BIG = 1.0e30


def wait(eng, sem, count):
    if not isinstance(count, int) or count > 0:
        eng.wait_ge(sem, count)


def adaln_moe(nc, x, xT, cond, cond_w, gate_w, gate_p, up_p, down_p, out):
    N, T = x.shape
    C = cond_w.shape[1]
    E, _, KD, F = gate_p.shape
    NT = N // P
    NG = NT // GROUP
    FC = -(-F // P)
    FR = F - (FC - 1) * P
    TILES = TOPK * NT + E - 1
    META = T
    ROW = T + 16
    assert 2 * C == P and KD * P == T and NG % 2 == 0 and (TILES - 3) % XSLOTS == 0

    x2s = nc.dram_tensor("x2s", [N + P, ROW], F32, kind="Internal")

    with ExitStack() as ctx:
        def sb(name, shape, dt=F32):
            return ctx.enter_context(nc.sbuf_tensor(name, shape, dt))

        def sem(name):
            return ctx.enter_context(nc.semaphore(name))

        bank = [ctx.enter_context(nc.psum_tensor(f"bank{i}", [P, 512], F32)) for i in range(8)]

        ident = sb("ident", [P, P])
        before = sb("before", [P, P], BF16)
        ones = sb("ones", [P, P], BF16)
        ones_f = sb("ones_f", [P, NT * E])
        lane = sb("lane", [P, 1])
        lane_pad = sb("lane_pad", [P, 1])
        rev_e = sb("rev_e", [P, GROUP, E])
        iota_e = sb("iota_e", [P, E])
        iota_r = sb("iota_r", [P, P], BF16)
        iota_q = sb("iota_q", [P, TILES + 1], BF16)
        iota_j = sb("iota_j", [P, TILES + 1])
        tile_m = sb("tile_m", [P, TOPK, NT])
        idx_lane = sb("idx_lane", [P, 1])
        cond_f = sb("cond_f", [P, NT])
        cond_i = sb("cond_i", [P, NT], I32)
        zero_row = sb("zero_row", [P, ROW])
        gw_sb = sb("gw_sb", [P, KD, E])

        w_gu = sb("w_gu", [P, E * KD * 2 * F])
        w_d = sb("w_d", [P, E * FC * T])
        w_gu5 = w_gu[:, :].rearrange("p (e c b f) -> p e c b f", e=E, c=KD, b=2)
        w_d4 = w_d[:, :].rearrange("p (e c t) -> p e c t", e=E, c=FC)

        x_in = [sb(f"x_in{s}", [P, GROUP, T]) for s in range(2)]
        xT_in = [sb(f"xT_in{s}", [P, KD, GROUP * P]) for s in range(2)]
        rows = [sb(f"rows{s}", [P, GROUP, ROW]) for s in range(2)]
        w_pick = [sb(f"w_pick{s}", [P, GROUP, C]) for s in range(2)]
        w_diag = [sb(f"w_diag{s}", [P, GROUP, P]) for s in range(2)]
        pick_idx = [sb(f"pick_idx{s}", [P, GROUP], I32) for s in range(2)]
        xg_sb = sb("xg_sb", [P, GROUP, E])
        lg = sb("lg", [P, GROUP, E])
        lg2 = sb("lg2", [P, GROUP, E])
        eq = sb("eq", [P, GROUP, E])
        cand = sb("cand", [P, GROUP, E])
        top = sb("top", [P, TOPK, GROUP])
        first = sb("first", [P, GROUP])
        gap = sb("gap", [P, GROUP])
        gap_e = sb("gap_e", [P, GROUP])
        den = sb("den", [P, GROUP])
        tw = sb("tw", [P, TOPK, GROUP])
        hot = [sb(f"hot{k}", [P, NT, E]) for k in range(TOPK)]
        member = sb("member", [P, E, NT], BF16)

        tot = sb("tot", [P, E * NT])
        cum = sb("cum", [P, E * NT])
        slot_a = sb("slot_a", [P, E * NT])
        slot_b = sb("slot_b", [P, E * NT])
        n_end = sb("n_end", [P, E])
        n_start = sb("n_start", [P, E])
        n_tok = sb("n_tok", [P, E])
        n_int = sb("n_int", [P, E], I32)
        n_til = sb("n_til", [P, E])
        t_end = sb("t_end", [P, E])
        off = sb("off", [P, E])
        prod = w_pick[0][:, :, :].rearrange("p g c -> p (g c)").rearrange("p (n e) -> p n e", e=E)
        entry = sb("entry", [P, TOPK * NT])
        entry_i = sb("entry_i", [P, TOPK * NT], I32)
        part_i = sb("part_i", [P, TOPK * NT], I32)
        ent_r = sb("ent_r", [P, TOPK * NT], BF16)
        ent_q = sb("ent_q", [P, TOPK * NT], BF16)
        ent_v = sb("ent_v", [P, TOPK * NT], BF16)
        ent_t = sb("ent_t", [P, TOPK * NT], BF16)
        QW = TILES + 1
        hot_r = [x_in[k][:, :, :].rearrange("p g t -> p (g t)").bitcast(BF16)[:, 0:NT * P]
                 .rearrange("p (n r) -> p n r", r=P) for k in range(TOPK)]
        hot_q3 = rows[0][:, :, :].rearrange("p g t -> p (g t)").bitcast(BF16)[:, 0:NT * QW] \
            .rearrange("p (n q) -> p n q", q=QW)
        val_q = [xT_in[k][:, :, :].rearrange("p g t -> p (g t)").bitcast(BF16)[:, 0:NT * QW]
                 .rearrange("p (n q) -> p n q", q=QW) for k in range(2)]
        list_f = sb("list_f", [P, QW])
        list_i = sb("list_i", [P, QW], I32)
        over = rows[1][:, :, :].rearrange("p g t -> p (g t)")[:, 0:QW * E].rearrange("p (q e) -> p q e", e=E)
        exp_f = sb("exp_f", [P, QW])
        exp_i = sb("exp_i", [P, QW], I32)
        exp_hot = sb("exp_hot", [P, QW, E], BF16)

        xg = [rows[0][:, s, :] for s in range(XSLOTS)]
        g_idx = [sb(f"g_idx{s}", [P, 1], I32) for s in range(XSLOTS)]
        s_idx = sb("s_idx", [P, 1], I32)
        xgT = [x_in[0][:, s, :] for s in range(2)]
        sg = [x_in[1][:, s, 0:F] for s in range(2)]
        h = [x_in[1][:, 2 + s, 0:F] for s in range(2)]
        hT = [x_in[0][:, 2 + s, 0:FC * P] for s in range(2)]
        tmp_e = sb("tmp_e", [P, E])
        tw_t = [sb(f"tw_t{s}", [P, 1]) for s in range(XSLOTS)]
        y = [rows[1][:, s, 0:T] for s in range(2)]

        ps_x2 = bank[0:4]
        ps_xg = bank[4][:, 0:GROUP * E].rearrange("p (g e) -> p g e", e=E)
        ps_lg = bank[5][:, 0:GROUP * E].rearrange("p (g e) -> p g e", e=E)
        ps_rank = bank[6][:, 0:E * NT]
        ps_tot = bank[7][:, 0:E * NT]
        ps_list = bank[5][:, 0:2 * QW]
        ps_g, ps_u = bank[0:2], bank[2:4]
        ps_y = bank[4:6]
        ps_xT = bank[6]
        ps_hT = bank[7]

        consts = sem("consts")
        gw_in = sem("gw_in")
        cond_in = sem("cond_in")
        idx_ready = sem("idx_ready")
        idx_copied = sem("idx_copied")
        zeroed = sem("zeroed")
        pads_out = sem("pads_out")
        x_ld = [sem(f"x_ld{s}") for s in range(2)]
        xT_ld = [sem(f"xT_ld{s}") for s in range(2)]
        pick_ld = [sem(f"pick_ld{s}") for s in range(2)]
        rows_st = [sem(f"rows_st{s}") for s in range(2)]
        x_st = [sem(f"x_st{s}") for s in range(2)]
        w_ld = sem("w_ld")
        diag_done = sem("diag_done")
        xg_ps = sem("xg_ps")
        xg_done = sem("xg_done")
        x2_ps = sem("x2_ps")
        x2_done = sem("x2_done")
        lg_ps = sem("lg_ps")
        gap_done = sem("gap_done")
        gap_exp = sem("gap_exp")
        rows_done = sem("rows_done")
        rt = sem("rt")
        ranks_ps = sem("ranks_ps")
        hot_done = sem("hot_done")
        list_ps = sem("list_ps")
        list_done = sem("list_done")
        pool_idx = sem("pool_idx")
        xg_ld = [sem(f"xg_ld{s}") for s in range(XSLOTS)]
        indexed = sem("indexed")
        xT_ps = sem("xT_ps")
        xT_done = sem("xT_done")
        gu_ps = sem("gu_ps")
        sg_done = sem("sg_done")
        h_done = sem("h_done")
        hT_ps = sem("hT_ps")
        hT_done = sem("hT_done")
        y_ps = sem("y_ps")
        tw_step = sem("tw_step")
        tw_done = sem("tw_done")
        y_done = sem("y_done")
        y_st = sem("y_st")

        POOL_CONSTS = 12
        block = ctx.enter_context(nc.Block())

        @block.sync
        def _(sp):
            sp.dma_start(gw_sb[:, :, :], gate_w).then_inc(gw_in, 16)

            def load(g, s, n):
                wait(sp, x2_ps, (g - 1) * GROUP)
                wait(sp, x_st[s], n * 16)
                sp.dma_start(x_in[s][:, :, :], x[bass.ds(g * GROUP * P, GROUP * P), :]
                             .rearrange("(i p) t -> p i t", p=P)).then_inc(x_ld[s], 16)
                sp.dma_start(xT_in[s][:, :, :], xT[:, bass.ds(g * GROUP * P, GROUP * P)]
                             .rearrange("(c p) n -> p c n", p=P)).then_inc(xT_ld[s], 16)

            def store(g, s, n):
                sp.wait_ge(x_ld[s], (n + 1) * 16)
                sp.dma_start(out[bass.ds(g * GROUP * P, GROUP * P), :]
                             .rearrange("(i p) t -> p i t", p=P), x_in[s][:, :, :]).then_inc(x_st[s], 16)
                sp.wait_ge(x2_done, (g + 1) * GROUP)
                sp.wait_ge(rows_done, g + 1)
                sp.dma_start(x2s[bass.ds(g * GROUP * P, GROUP * P), :]
                             .rearrange("(i p) t -> p i t", p=P), rows[s][:, :, :]).then_inc(rows_st[s], 16)

            def weights(e):
                sp.dma_start(w_gu5[:, e, :, 0, :], gate_p[e]).then_inc(w_ld, 16)
                sp.dma_start(w_gu5[:, e, :, 1, :], up_p[e]).then_inc(w_ld, 16)
                sp.dma_start(w_d4[:, e, 0:FC - 1, :], down_p[e, 0:(FC - 1) * P, :]
                             .rearrange("(c p) t -> p c t", p=P)).then_inc(w_ld, 16)
                sp.dma_start(w_d4[0:FR, e, FC - 1, :], down_p[e, (FC - 1) * P:F, :]).then_inc(w_ld, 16)

            load(0, 0, 0)
            load(1, 1, 0)
            with sp.Fori(0, NG // 2 - 1) as n:
                for s in range(2):
                    store(2 * n + s, s, n)
                    load(2 * n + s + 2, s, n + 1)
            for s in range(2):
                store(NG - 2 + s, s, NG // 2 - 1)
            for e in range(E):
                weights(e)
            sp.wait_ge(zeroed, 1)
            sp.dma_start(x2s[N:N + P, :], zero_row[:, :]).then_inc(pads_out, 16)
            sp.dma_start(out[N:N + P, :], zero_row[:, 0:T]).then_inc(pads_out, 16)

        @block.gpsimd
        def _(pool):
            dmas = pool.alloc_register("dmas")
            pool.reg_mov(dmas, 0)

            def stand():
                pool.sem_inc(indexed, 1)

            pool.memset(ident[:, :], 0.0).then_inc(zeroed, 1)
            pool.memset(before[:, :], 1.0).then_inc(zeroed, 1)
            pool.memset(ones[:, :], 1.0).then_inc(consts, 1)
            pool.iota(lane[:, :], [[0, 1]], base=0, channel_multiplier=1,
                      allow_small_or_imprecise_dtypes=True).then_inc(consts, 1)
            pool.iota(lane_pad[:, :], [[0, 1]], base=N, channel_multiplier=1,
                      allow_small_or_imprecise_dtypes=True).then_inc(consts, 1)
            pool.iota(rev_e[:, :, :], [[0, GROUP], [-1, E]], base=E, channel_multiplier=0,
                      allow_small_or_imprecise_dtypes=True).then_inc(consts, 1)
            pool.iota(iota_e[:, :], [[1, E]], base=0, channel_multiplier=0,
                      allow_small_or_imprecise_dtypes=True).then_inc(consts, 1)
            pool.iota(iota_r[:, :], [[1, P]], base=0, channel_multiplier=0,
                      allow_small_or_imprecise_dtypes=True).then_inc(consts, 1)
            pool.iota(iota_q[:, :], [[1, QW]], base=0, channel_multiplier=0,
                      allow_small_or_imprecise_dtypes=True).then_inc(consts, 1)
            pool.iota(iota_j[:, :], [[1, QW]], base=0, channel_multiplier=0,
                      allow_small_or_imprecise_dtypes=True).then_inc(consts, 1)
            pool.iota(tile_m[:, :, :], [[0, TOPK], [1, NT]], base=-NT, channel_multiplier=0,
                      allow_small_or_imprecise_dtypes=True).then_inc(consts, 1)
            for s in range(2):
                pool.memset(w_diag[s][:, :, :], 0.0).then_inc(consts, 1)
            pool.wait_ge(zeroed, 3)
            pool.affine_select(out=ident[:, :], in_=ident[:, :], compare_op=ALU.not_equal, fill=1.0, base=0,
                               pattern=[[-1, P]], channel_multiplier=1).then_inc(consts, 1)
            pool.affine_select(out=before[:, :], in_=before[:, :], compare_op=ALU.is_ge, fill=0.0, base=-1,
                               pattern=[[1, P]], channel_multiplier=-1).then_inc(consts, 1)

            pool.wait_ge(idx_ready, 2)
            def pick(g, s, n):
                wait(pool, pick_ld[s], n * 16 * GROUP)
                wait(pool, diag_done, 2 * n)
                pool.tensor_copy(pick_idx[s][:, :], cond_i[:, bass.ds(g * GROUP, GROUP)]).then_inc(idx_copied, 1)
                wait(pool, idx_copied, g + 1)
                stand()
                for i in range(GROUP):
                    pool.indirect_dma_start(
                        out=w_pick[s][:, i, :], out_offset=None, in_=cond_w,
                        in_offset=bass.IndirectOffsetOnAxis(ap=pick_idx[s][:, i:i + 1], axis=0),
                    ).then_inc(pick_ld[s], 16)

            for s in range(2):
                pick(s, s, 0)
            with pool.Fori(1, NG // 2) as n:
                for s in range(2):
                    pick(2 * n + s, s, n)

            pool.wait_ge(list_done, 1)
            pool.wait_ge(pads_out, 32)
            for s in range(2):
                pool.wait_ge(rows_st[s], 16 * NG // 2)
                pool.wait_ge(x_st[s], 16 * NG // 2)

            def gather(j, u, copies):
                pool.tensor_copy(g_idx[u][:, :], list_i[:, bass.ds(j, 1)]).then_inc(pool_idx, 1)
                pool.wait_ge(pool_idx, copies)
                stand()
                pool.indirect_dma_start(
                    out=xg[u], out_offset=None, in_=x2s[:, :],
                    in_offset=bass.IndirectOffsetOnAxis(ap=g_idx[u][:, :], axis=0)).then_inc(xg_ld[u], 16)

            def scatter(j, s, copies):
                wait(pool, y_st, 16 * j)
                pool.tensor_copy(s_idx[:, :], list_i[:, bass.ds(j, 1)]).then_inc(pool_idx, 1)
                pool.wait_ge(pool_idx, copies)
                pool.wait_ge(y_done, j + 1)
                stand()
                pool.indirect_dma_start(
                    out=out[:, :], out_offset=bass.IndirectOffsetOnAxis(ap=s_idx[:, :], axis=0),
                    in_=y[s], in_offset=None, compute_op=ALU.add).then_inc(y_st, 16)

            def step(j, u, more):
                scatter(j, u % 2, XSLOTS + 2 * j + 1)
                if more:
                    pool.wait_ge(xT_ps, j + 1)
                    pool.wait_ge(tw_done, j + 1)
                    gather(j + XSLOTS, u, XSLOTS + 2 * j + 2)

            for u in range(XSLOTS):
                gather(u, u, u + 1)
            for u in range(XSLOTS):
                step(u, u, True)
            with pool.Fori(1, (TILES - XSLOTS) // XSLOTS) as i:
                for u in range(XSLOTS):
                    step(XSLOTS * i + u, u, True)
            J0 = (TILES - XSLOTS) // XSLOTS * XSLOTS
            for j in range(J0, TILES - XSLOTS):
                step(j, j % XSLOTS, True)
            c = XSLOTS + 2 * (TILES - XSLOTS)
            for j in range(TILES - XSLOTS, TILES):
                c += 1
                scatter(j, j % 2, c)
            pool.wait_ge(y_st, 16 * TILES)

        @block.scalar
        def _(act):
            with nc.allow_non_contiguous_dma(reason="ids of every other batch entry"):
                for b in range(2):
                    act.dma_start(cond_i[b * C:(b + 1) * C, :], cond[b:b + 1, :].to_broadcast([C, NT])).then_inc(cond_in, 16)
            act.wait_ge(consts, POOL_CONSTS)
            def condition(g, s, n):
                act.wait_ge(pick_ld[s], (n + 1) * 16 * GROUP)
                wait(act, lg_ps, 2 * n)
                for b in range(2):
                    c = slice(b * C, (b + 1) * C)
                    copy = act.activation(w_diag[s][c, :, c], w_pick[s][c, :, :], ACT.Copy)
                copy.then_inc(diag_done, 1)
                act.wait_ge(xg_ps, g + 1)
                act.activation(xg_sb[:, :, :], ps_xg, ACT.Copy).then_inc(xg_done, 1)
                wait(act, rows_st[s], n * 16)
                for i in range(GROUP):
                    act.wait_ge(x2_ps, g * GROUP + i + 1)
                    act.activation(rows[s][:, i, 0:T], ps_x2[i][:, :], ACT.Copy).then_inc(x2_done, 1)
                act.wait_ge(gap_done, g + 1)
                act.activation(gap_e[:, :], gap[:, :], ACT.Exp).then_inc(gap_exp, 1)

            for s in range(2):
                condition(s, s, 0)
            with act.Fori(1, NG // 2) as n:
                for s in range(2):
                    condition(2 * n + s, s, n)

            def evac_x(j, s):
                act.wait_ge(xT_ps, j + 1)
                act.activation(xgT[s], ps_xT[:, :], ACT.Copy).then_inc(xT_done, 1)

            def evac_h(j, s):
                act.wait_ge(hT_ps, j + 1)
                act.activation(hT[s][:, 0:(FC - 1) * P], ps_hT[:, 0:(FC - 1) * P], ACT.Copy).then_inc(hT_done, 1)
                act.activation(hT[s][0:FR, (FC - 1) * P:FC * P], ps_hT[0:FR, (FC - 1) * P:FC * P],
                               ACT.Copy).then_inc(hT_done, 1)

            def silu(j, s):
                act.wait_ge(gu_ps, j + 1)
                act.activation(sg[s], ps_g[s][:, 0:F], ACT.Silu).then_inc(sg_done, 1)

            def step(j, u, last=False):
                s = u % 2
                if u:
                    wait(act, y_ps, j - 2)
                    evac_h(j - 1, 1 - s)
                if not last:
                    wait(act, gu_ps, j)
                    evac_x(j + 1, 1 - s)
                wait(act, h_done, j - 1)
                silu(j, s)

            evac_x(0, 0)
            for j in range(3):
                step(j, j)
            with act.Fori(0, (TILES - 3) // XSLOTS - 1) as i:
                for u in range(XSLOTS):
                    step(XSLOTS * i + u + 3, u + 3)
            for j in range(TILES - XSLOTS, TILES):
                step(j, j, j == TILES - 1)
            act.wait_ge(y_ps, TILES - 2)
            evac_h(TILES - 1, (TILES - 1) % 2)

        @block.tensor
        def _(pe):
            pe.wait_ge(gw_in, 16)
            def condition(g, s, n):
                pe.wait_ge(xT_ld[s], (n + 1) * 16)
                wait(pe, xg_done, g)
                for i in range(GROUP):
                    for c in range(KD):
                        mm = pe.matmul(ps_xg[:, i, :], xT_in[s][:, c, i * P:(i + 1) * P], gw_sb[:, c, :],
                                       start=(c == 0), stop=(c == KD - 1))
                mm.then_inc(xg_ps, 1)
                pe.wait_ge(diag_done, g + 1)
                pe.wait_ge(x_ld[s], (n + 1) * 16)
                for i in range(GROUP):
                    wait(pe, x2_done, (g - 1) * GROUP + i + 1)
                    pe.matmul(ps_x2[i][:, :], w_diag[s][:, i, :], x_in[s][:, i, :], start=True,
                              stop=True).then_inc(x2_ps, 1)
                pe.wait_ge(xg_done, g + 1)
                wait(pe, rows_done, g)
                for i in range(GROUP):
                    mm = pe.matmul(ps_lg[:, i, :], w_diag[s][:, i, :], xg_sb[:, i, :], start=True, stop=True)
                mm.then_inc(lg_ps, 1)

            for s in range(2):
                condition(s, s, 0)
            with pe.Fori(1, NG // 2) as n:
                for s in range(2):
                    condition(2 * n + s, s, n)
            pe.wait_ge(rows_done, NG)
            mem = member[:, :, :].rearrange("p e n -> p (e n)")
            pe.matmul(ps_rank, before[:, :], mem, start=True, stop=True)
            pe.matmul(ps_tot, ones[:, :], mem, start=True, stop=True).then_inc(ranks_ps, 1)
            for k in range(TOPK):
                pe.wait_ge(hot_done, k + 1)
                for t in range(NT):
                    for v in range(2):
                        pe.matmul(ps_list[:, v * QW:(v + 1) * QW], hot_r[k][:, t, :], val_q[v][:, t, :],
                                  start=(k == 0 and t == 0 and v == 0), stop=(k == TOPK - 1 and t == NT - 1),
                                  skip_group_check=True).then_inc(list_ps, 1)
            pe.wait_ge(list_done, 1)
            pe.wait_ge(w_ld, 16 * 4 * E)

            def transpose_x(j, u, n):
                pe.wait_ge(xg_ld[u % XSLOTS], 16 * (n + 1))
                wait(pe, xT_done, j)
                for c in range(KD):
                    tr = pe.transpose(ps_xT[:, c * P:(c + 1) * P], xg[u % XSLOTS][:, c * P:(c + 1) * P], ident[:, :])
                tr.then_inc(xT_ps, 1)

            def gate_up(j, s, e, chunks):
                if 0 in chunks:
                    pe.wait_ge(xT_done, j + 1)
                    wait(pe, h_done, j - 1)
                for c in chunks:
                    for b, ps in ((0, ps_g), (1, ps_u)):
                        mm = pe.matmul(ps[s][:, 0:F], xgT[s][:, c * P:(c + 1) * P],
                                       w_gu[:, bass.ds(e * (KD * 2 * F) + (2 * c + b) * F, F)],
                                       start=(c == 0), stop=(c == KD - 1))
                if KD - 1 in chunks:
                    mm.then_inc(gu_ps, 1)

            def transpose_h(j, s):
                pe.wait_ge(h_done, j + 1)
                wait(pe, hT_done, 2 * j)
                for c in range(FC):
                    w = P if c < FC - 1 else FR
                    tr = pe.transpose(ps_hT[0:w, c * P:(c + 1) * P], h[s][:, c * P:c * P + w], ident[:, :])
                tr.then_inc(hT_ps, 1)

            def down(j, s, e):
                pe.wait_ge(hT_done, 2 * (j + 1))
                wait(pe, y_done, j - 1)
                for c in range(FC):
                    w = P if c < FC - 1 else FR
                    mm = pe.matmul(ps_y[s][:, :], hT[s][0:w, c * P:(c + 1) * P],
                                   w_d[0:w, bass.ds(e * (FC * T) + c * T, T)], start=(c == 0), stop=(c == FC - 1))
                mm.then_inc(y_ps, 1)

            def expert(j):
                return pe.value_load(exp_i[0:1, bass.ds(j, 1)], min_val=0, max_val=E - 1)

            def step(j, u, n_next, last=False):
                s = u % 2
                e = expert(j)
                gate_up(j, s, e, range(0, KD // 2))
                if not (isinstance(j, int) and j == 0):
                    transpose_h(j - 1, 1 - s)
                if not last:
                    transpose_x(j + 1, u + 1, n_next)
                gate_up(j, s, e, range(KD // 2, KD))
                if not (isinstance(j, int) and j == 0):
                    down(j - 1, 1 - s, expert(j - 1))

            transpose_x(0, 0, 0)
            step(0, 0, 0)
            step(1, 1, 0)
            step(2, 2, 0)
            with pe.Fori(0, (TILES - 3) // XSLOTS - 1) as i:
                for u in range(XSLOTS):
                    step(XSLOTS * i + u + 3, u + 3, i + 1 if u == 0 else i + 1)
            for j in range(TILES - XSLOTS, TILES):
                step(j, j % XSLOTS + XSLOTS, (j + 1) // XSLOTS, j == TILES - 1)
            transpose_h(TILES - 1, (TILES - 1) % 2)
            down(TILES - 1, (TILES - 1) % 2, expert(TILES - 1))

        @block.vector
        def _(dve):
            done = [0]

            def link(ins, base=0):
                done[0] += 1
                ins.then_inc(rt, 1)
                dve.wait_ge(rt, base + done[0])

            link(dve.memset(zero_row[:, :], 0.0))
            for s in range(2):
                link(dve.memset(rows[s][:, :, :], 0.0))
            dve.memset(ones_f[:, :], 1.0).then_inc(zeroed, 1)
            dve.wait_ge(cond_in, 32)
            dve.wait_ge(consts, POOL_CONSTS)
            link(dve.tensor_copy(cond_f[:, :], cond_i[:, :]))
            link(dve.tensor_scalar(idx_lane[:, :], lane[:, :], float(C), -float(C), ALU.is_ge, ALU.mult))
            link(dve.tensor_tensor(idx_lane[:, :], idx_lane[:, :], lane[:, :], ALU.add))
            dve.tensor_scalar(cond_i[:, :], cond_f[:, :], float(C), idx_lane[:, 0:1], ALU.mult,
                              ALU.add).then_inc(idx_ready, 2)

            pre = done[0]
            PER = 19
            def route(g, s, n):
                done[0] = 0
                base = g * PER + pre

                def own(ins):
                    link(ins, base)

                def spread(a):
                    return a.unsqueeze(2).to_broadcast([P, GROUP, E])

                dve.wait_ge(lg_ps, g + 1)
                own(dve.tensor_copy(lg[:, :, :], ps_lg))
                src = lg
                for k in range(TOPK):
                    hk = hot[k][:, bass.ds(g * GROUP, GROUP), :]
                    own(dve.tensor_reduce(top[:, k, :], src[:, :, :], AX.X, ALU.max))
                    own(dve.tensor_tensor(eq[:, :, :], src[:, :, :], spread(top[:, k, :]), ALU.is_equal))
                    own(dve.tensor_tensor(cand[:, :, :], eq[:, :, :], rev_e[:, :, :], ALU.mult))
                    own(dve.tensor_reduce(first[:, :], cand[:, :, :], AX.X, ALU.max))
                    own(dve.tensor_tensor(hk, rev_e[:, :, :], spread(first[:, :]), ALU.is_equal))
                    if k == 0:
                        own(dve.scalar_tensor_tensor(out=lg2[:, :, :], in0=hk, scalar=-BIG, in1=lg[:, :, :],
                                                     op0=ALU.mult, op1=ALU.add))
                        src = lg2
                wait(dve, gap_exp, g)
                dve.tensor_tensor(gap[:, :], top[:, 1, :], top[:, 0, :], ALU.subtract).then_inc(gap_done, 1)
                dve.wait_ge(gap_exp, g + 1)
                own(dve.tensor_scalar(den[:, :], gap_e[:, :], 1.0, None, ALU.add))
                own(dve.reciprocal(tw[:, 0, :], den[:, :]))
                own(dve.tensor_tensor(tw[:, 1, :], gap_e[:, :], tw[:, 0, :], ALU.mult))
                h0 = hot[0][:, bass.ds(g * GROUP, GROUP), :]
                h1 = hot[1][:, bass.ds(g * GROUP, GROUP), :]
                own(dve.tensor_tensor(eq[:, :, :], h0, spread(tw[:, 0, :]), ALU.mult))
                own(dve.tensor_tensor(cand[:, :, :], h1, spread(tw[:, 1, :]), ALU.mult))
                own(dve.tensor_tensor(member[:, :, bass.ds(g * GROUP, GROUP)].rearrange("p e n -> p n e"),
                                      h0, h1, ALU.add))
                wait(dve, rows_st[s], n * 16)
                assert done[0] == PER - 1, done[0]
                own(dve.tensor_tensor(rows[s][:, :, META:META + E], eq[:, :, :], cand[:, :, :], ALU.add))
                dve.sem_inc(rows_done, 1)

            for s in range(2):
                route(s, s, 0)
            with dve.Fori(1, NG // 2) as n:
                for s in range(2):
                    route(2 * n + s, s, n)

            done[0] = pre + NG * PER
            dve.wait_ge(ranks_ps, 1)
            link(dve.tensor_copy(tot[:, :], ps_tot))
            link(dve.tensor_tensor_scan(cum[:, :], ones_f[:, :], tot[:, :], 0.0, ALU.mult, ALU.add))
            link(dve.tensor_tensor(slot_a[:, :], cum[:, :], tot[:, :], ALU.subtract))
            link(dve.tensor_tensor(slot_b[:, :], ps_rank, slot_a[:, :], ALU.add))
            ends = cum[:, :].rearrange("p (e n) -> p e n", e=E)[:, :, NT - 1]
            link(dve.memset(n_start[:, 0:1], 0.0))
            link(dve.tensor_copy(n_end[:, :], ends))
            link(dve.tensor_copy(n_start[:, 1:E], n_end[:, 0:E - 1]))
            link(dve.tensor_tensor(n_tok[:, :], n_end[:, :], n_start[:, :], ALU.subtract))
            link(dve.tensor_scalar(n_int[:, :], n_tok[:, :], float(P - 1), None, ALU.add))
            link(dve.tensor_scalar(n_int[:, :], n_int[:, :], 7, None, ALU.logical_shift_right))
            link(dve.tensor_copy(n_til[:, :], n_int[:, :]))
            link(dve.tensor_tensor_scan(t_end[:, :], ones_f[:, 0:E], n_til[:, :], 0.0, ALU.mult, ALU.add))
            link(dve.tensor_tensor(off[:, :], t_end[:, :], n_til[:, :], ALU.subtract))
            link(dve.tensor_scalar(off[:, :], off[:, :], float(P), None, ALU.mult))
            link(dve.tensor_tensor(off[:, :], off[:, :], n_start[:, :], ALU.subtract))
            link(dve.tensor_tensor(slot_a[:, :].rearrange("p (e n) -> p e n", e=E),
                                   slot_b[:, :].rearrange("p (e n) -> p e n", e=E),
                                   off[:, :].unsqueeze(2).to_broadcast([P, E, NT]), ALU.add))
            slot_ne = slot_a[:, :].rearrange("p (e n) -> p n e", e=E)
            for k in range(TOPK):
                link(dve.tensor_tensor(prod, hot[k][:, :, :], slot_ne, ALU.mult))
                link(dve.tensor_reduce(entry[:, k * NT:(k + 1) * NT], prod, AX.X, ALU.add))
            link(dve.tensor_copy(entry_i[:, :], entry[:, :]))
            link(dve.tensor_scalar(part_i[:, :], entry_i[:, :], 7, None, ALU.logical_shift_right))
            link(dve.tensor_copy(ent_q[:, :], part_i[:, :]))
            link(dve.tensor_scalar(part_i[:, :], entry_i[:, :], P - 1, None, ALU.bitwise_and))
            link(dve.tensor_copy(ent_r[:, :], part_i[:, :]))
            link(dve.tensor_scalar(ent_v[:, :], ent_r[:, :], -1.0, lane[:, 0:1], ALU.mult, ALU.add))
            link(dve.tensor_copy(ent_t[:, :], tile_m[:, :, :].rearrange("p k n -> p (k n)")))
            for s in range(2):
                dve.wait_ge(rows_st[s], 16 * NG // 2)
                dve.wait_ge(x_st[s], 16 * NG // 2)
            for k in range(TOPK):
                part = slice(k * NT, (k + 1) * NT)
                if k:
                    dve.wait_ge(list_ps, 2 * NT)
                link(dve.tensor_tensor(hot_r[k], iota_r[:, :].unsqueeze(1).to_broadcast([P, NT, P]),
                                       ent_r[:, part].unsqueeze(2).to_broadcast([P, NT, P]), ALU.is_equal))
                link(dve.tensor_tensor(hot_q3, iota_q[:, :].unsqueeze(1).to_broadcast([P, NT, QW]),
                                       ent_q[:, part].unsqueeze(2).to_broadcast([P, NT, QW]), ALU.is_equal))
                link(dve.tensor_tensor(val_q[0], hot_q3,
                                       ent_v[:, part].unsqueeze(2).to_broadcast([P, NT, QW]), ALU.mult))
                link(dve.tensor_tensor(val_q[1], hot_q3,
                                       ent_t[:, part].unsqueeze(2).to_broadcast([P, NT, QW]), ALU.mult))
                dve.sem_inc(hot_done, 1)
            link(dve.tensor_tensor(over, iota_j[:, :].unsqueeze(2).to_broadcast([P, QW, E]),
                                   t_end[:, :].unsqueeze(1).to_broadcast([P, QW, E]), ALU.is_ge))
            link(dve.tensor_reduce(exp_f[:, :], over, AX.X, ALU.add))
            link(dve.tensor_scalar(exp_f[:, :], exp_f[:, :], float(E - 1), None, ALU.min))
            link(dve.tensor_copy(exp_i[:, :], exp_f[:, :]))
            link(dve.tensor_tensor(exp_hot[:, :, :], iota_e[:, :].unsqueeze(1).to_broadcast([P, QW, E]),
                                   exp_f[:, :].unsqueeze(2).to_broadcast([P, QW, E]), ALU.is_equal))
            dve.wait_ge(list_ps, 2 * TOPK * NT)
            link(dve.tensor_scalar(list_f[:, :], ps_list[:, 0:QW], lane_pad[:, 0:1], None, ALU.add))
            link(dve.scalar_tensor_tensor(out=list_f[:, :], in0=ps_list[:, QW:2 * QW], scalar=float(P),
                                          in1=list_f[:, :], op0=ALU.mult, op1=ALU.add))
            link(dve.tensor_copy(list_i[:, :], list_f[:, :]))
            dve.sem_inc(list_done, 1)

            def weight(j, u, n):
                dve.wait_ge(xg_ld[u], 16 * (n + 1))
                wait(dve, tw_done, j)
                dve.tensor_tensor(tmp_e[:, :], xg[u][:, META:META + E],
                                  exp_hot[:, bass.ds(j, 1), :].rearrange("p a e -> p (a e)"), ALU.mult).then_inc(tw_step, 1)
                dve.wait_ge(tw_step, j + 1)
                dve.tensor_reduce(tw_t[u][:, :], tmp_e[:, :], AX.X, ALU.add).then_inc(tw_done, 1)

            def hidden(j, s):
                dve.wait_ge(sg_done, j + 1)
                wait(dve, hT_ps, j - 1)
                dve.tensor_tensor(h[s], ps_u[s][:, 0:F], sg[s], ALU.mult).then_inc(h_done, 1)

            def scaled(j, u):
                s = u % 2
                dve.wait_ge(y_ps, j + 1)
                dve.wait_ge(tw_done, j + 1)
                wait(dve, y_st, 16 * (j - 1))
                dve.tensor_scalar(y[s], ps_y[s][:, :], tw_t[u][:, 0:1], None, ALU.mult).then_inc(y_done, 1)

            def step(j, u, n):
                weight(j, u, n)
                hidden(j, u % 2)
                if not (isinstance(j, int) and j == 0):
                    scaled(j - 1, (u - 1) % XSLOTS)

            for j in range(3):
                step(j, j, 0)
            with dve.Fori(0, (TILES - 3) // XSLOTS) as i:
                for u in range(XSLOTS):
                    step(XSLOTS * i + u + 3, (u + 3) % XSLOTS, i + (u + 3) // XSLOTS)
            scaled(TILES - 1, (TILES - 1) % XSLOTS)


def kernel(x, itok_B_1_198, L0_cond_weights, L0_ffn_gate_w, L0_ffn_gate_proj, L0_ffn_up_proj, L0_ffn_down_proj):
    import numpy as np
    import concourse.bacc as bacc
    from concourse.bass_utils import run_bass_kernel_spmd

    B, C, T = x.shape
    E, F, _ = L0_ffn_gate_proj.shape
    N = B * C
    flat = np.ascontiguousarray(x).reshape(N, T)

    def chunked(w):
        return np.ascontiguousarray(np.transpose(np.asarray(w).reshape(E, F, T // 128, 128), (0, 3, 2, 1)))

    arrays = {
        "x": flat,
        "xT": np.ascontiguousarray(flat.T),
        "cond": np.ascontiguousarray(np.asarray(itok_B_1_198).reshape(B // 2, 2).T),
        "cond_w": np.ascontiguousarray(L0_cond_weights).reshape(-1, C),
        "gate_w": np.ascontiguousarray(np.transpose(np.asarray(L0_ffn_gate_w).reshape(E, T // 128, 128), (2, 1, 0))),
        "gate_p": chunked(L0_ffn_gate_proj),
        "up_p": chunked(L0_ffn_up_proj),
        "down_p": np.ascontiguousarray(np.transpose(np.asarray(L0_ffn_down_proj), (0, 2, 1))),
    }
    nc = bacc.Bacc("TRN2", target_bir_lowering=False, num_devices=1)
    args = [nc.dram_tensor(name, a.shape, mybir.dt.from_np(a.dtype), kind="ExternalInput").ap()
            for name, a in arrays.items()]
    out = nc.dram_tensor("out", (N + 128, T), F32, kind="ExternalOutput").ap()
    adaln_moe(nc, *args, out)
    r = run_bass_kernel_spmd(nc, [arrays], core_ids=[0])
    return r.results[0]["out"][0:N].reshape(B, C, T)
```

```python
from contextlib import ExitStack

import concourse.bass as bass
from concourse import mybir

P = 128
ALU = mybir.AluOpType
ACT = mybir.ActivationFunctionType
AX = mybir.AxisListType
F32 = mybir.dt.float32
BF16 = mybir.dt.bfloat16
F16 = mybir.dt.float16
I32 = mybir.dt.int32

TOPK = 2
GROUP = 4
XSLOTS = 4
BIG = 1.0e30

PRODUCTS = ((0, 0), (0, 1), (1, 0))
MANT = float(1 << 23)
N2_MIN = 67 * MANT
S_EXP = 205 * MANT
INV_EXP = 49 * MANT


def wait(eng, sem, count):
    if not isinstance(count, int) or count > 0:
        eng.wait_ge(sem, count)


def adaln_moe(nc, x, xT, cond, cond_w, gate_w, weights, F, out):
    N, T = x.shape
    C = cond_w.shape[1]
    E, W = weights.shape[0], weights.shape[2]
    KD = T // P
    NT = N // P
    NG = NT // GROUP
    FC = -(-F // P)
    FR = F - (FC - 1) * P
    TILES = TOPK * NT + E - 1
    META = T
    GU, DN = KD * 2 * F, FC * T
    ROW = T + 16
    assert 2 * C == P and KD * P == T and NG == E == 8 and FC == 3 and (TILES - 3) % XSLOTS == 0

    x2s = nc.dram_tensor("x2s", [N + P, ROW], F32, kind="Internal")

    with ExitStack() as ctx:
        def sb(name, shape, dt=F32):
            return ctx.enter_context(nc.sbuf_tensor(name, shape, dt))

        def sem(name):
            return ctx.enter_context(nc.semaphore(name))

        bank = [ctx.enter_context(nc.psum_tensor(f"bank{i}", [P, 512], F32)) for i in range(8)]

        before = sb("before", [P, P], BF16)
        ones = sb("ones", [P, P], BF16)
        ones_f = sb("ones_f", [P, NT * E])
        ident_h = sb("ident_h", [P, P], F16)
        lane = sb("lane", [P, 1])
        lane_pad = sb("lane_pad", [P, 1])
        rev_e = sb("rev_e", [P, NT, E])
        iota_e = sb("iota_e", [P, E])
        iota_r = sb("iota_r", [P, P], BF16)
        iota_q = sb("iota_q", [P, TILES + 1], BF16)
        iota_j = sb("iota_j", [P, TILES + 1])
        tile_m = sb("tile_m", [P, TOPK, NT])
        idx_lane = sb("idx_lane", [P, 1])
        cond_f = sb("cond_f", [P, NT])
        cond_i = sb("cond_i", [P, NT], I32)
        spare = sb("spare", [P, 2 * FC * P])
        zero_row = spare[:, 0:ROW]
        gw_sb = sb("gw_sb", [P, KD, E])

        w_res = sb("w_res", [P, E * W])
        w_16 = w_res[:, :].bitcast(F16)

        PARTS = tuple(enumerate(((0, GU), (GU, DN))))
        HN = NT // 2
        QW = TILES + 1
        A1 = max(NT * P, W)
        A2 = A1 + (HN * P + 3 * HN * QW) // 2
        A3 = A2 + 4 * NT * E
        arena = sb("arena", [P, max(A3 + 3 * NT * E, A1 + 8 * T)])
        w_last = arena[:, 0:W]

        XT_SLOTS = 4
        X0 = E * W - XT_SLOTS * GROUP * T

        def x_slot(g):
            return (g, 1) if g < 2 else (2 + g % 2, g // 2)
        PICKS = 4
        w_pick = [arena[:, A1 + s * GROUP * C:A1 + (s + 1) * GROUP * C].rearrange("p (g c) -> p g c", c=C)
                  for s in range(PICKS)]
        dump, dump_last = [arena[:, at:at + GU // 2].bitcast(BF16) for at in (A1 + PICKS * GROUP * C, A2)]
        rows = [sb(f"rows{s}", [P, GROUP, ROW]) for s in range(2)]
        pick_idx = [sb(f"pick_idx{s}", [P, GROUP], I32) for s in range(PICKS)]
        xT_in = [rows[s][:, :, :].rearrange("p g t -> p (g t)")[:, 0:KD * GROUP * P]
                 .rearrange("p (c n) -> p c n", c=KD) for s in range(2)]
        xg_sb = sb("xg_sb", [P, NT, E])
        n2_x = sb("n2_x", [P, GROUP])
        k_x = sb("k_x", [P, GROUP], I32)
        s_x = sb("s_x", [P, GROUP], I32)
        n2_w = [sb(f"n2_w{s}", [P, 2]) for s in range(2)]
        k_w = sb("k_w", [P, 2], I32)
        s_w = [sb(f"s_w{s}", [P, 2], I32) for s in range(2)]
        inv_w = sb("inv_w", [P, 2, E], I32)
        inv_t = sb("inv_t", [P, 2, TILES + 1])
        lg, lg2, eq, cand = [arena[:, A2 + i * NT * E:A2 + (i + 1) * NT * E].rearrange("p (n e) -> p n e", e=E)
                             for i in range(4)]
        top = sb("top", [P, TOPK, NT])
        first = sb("first", [P, NT])
        gap = sb("gap", [P, NT])
        gap_e = sb("gap_e", [P, NT])
        den = sb("den", [P, NT])
        tw = sb("tw", [P, TOPK, NT])
        tw_all = sb("tw_all", [P, NT, E])
        hot = [sb(f"hot{k}", [P, NT, E]) for k in range(TOPK)]
        member = sb("member", [P, E, NT], BF16)

        tot, cum = arena[:, A3:A3 + E * NT], arena[:, A3 + E * NT:A3 + 2 * E * NT]
        slots = tot
        n_end = sb("n_end", [P, E])
        n_start = sb("n_start", [P, E])
        n_tok = sb("n_tok", [P, E])
        n_int = sb("n_int", [P, E], I32)
        n_til = sb("n_til", [P, E])
        t_end = sb("t_end", [P, E])
        off = sb("off", [P, E])
        prod = arena[:, A3 + 2 * E * NT:A3 + 3 * E * NT].rearrange("p (n e) -> p n e", e=E)
        entry = sb("entry", [P, TOPK * NT])
        entry_i = sb("entry_i", [P, TOPK * NT], I32)
        part_i = sb("part_i", [P, TOPK * NT], I32)
        ent_r = sb("ent_r", [P, TOPK * NT], BF16)
        ent_q = sb("ent_q", [P, TOPK * NT], BF16)
        ent_v = sb("ent_v", [P, TOPK * NT], BF16)
        ent_t = sb("ent_t", [P, TOPK * NT], BF16)
        one_hots = arena[:, A1:A2].bitcast(BF16)
        hot_r = one_hots[:, 0:HN * P].rearrange("p (n r) -> p n r", r=P)
        hot_q, val_t, val_p = [one_hots[:, HN * P + i * HN * QW:HN * P + (i + 1) * HN * QW]
                               .rearrange("p (n q) -> p n q", q=QW) for i in range(3)]
        list_f = sb("list_f", [P, QW])
        list_i = sb("list_i", [P, QW], I32)
        over = arena[:, A2:A2 + QW * E].rearrange("p (q e) -> p q e", e=E)
        exp_f = sb("exp_f", [P, QW])
        exp_i = sb("exp_i", [P, QW], I32)
        exp_hot = sb("exp_hot", [P, QW, E], BF16)

        xg = [rows[0][:, s, :] for s in range(XSLOTS)]
        g_idx = [sb(f"g_idx{s}", [P, 1], I32) for s in range(XSLOTS)]
        s_idx = sb("s_idx", [P, 1], I32)
        xgT = [arena[:, A1 + s * T:A1 + (s + 1) * T].bitcast(F16).rearrange("p (v c n) -> p v c n", v=2, c=KD)
               for s in range(2)]
        sg = [arena[:, A1 + (2 + s) * T:A1 + (2 + s) * T + F] for s in range(2)]
        h = [arena[:, A1 + (4 + s) * T:A1 + (4 + s) * T + F] for s in range(2)]
        sq = arena[:, A1 + 6 * T:A1 + 6 * T + F]
        h_half = [part.bitcast(F16).rearrange("p (v f) -> p v f", v=2)
                  for part in (arena[:, A1 + 7 * T:A1 + 7 * T + FC * P], spare[:, FC * P:2 * FC * P])]
        hT = [part.bitcast(F16).rearrange("p (v c n) -> p v c n", v=2, c=FC)
              for part in (spare[:, 0:FC * P], rows[1][:, 2, 0:FC * P])]
        tmp_e = sb("tmp_e", [P, E])
        sc_gu = [sb(f"sc_gu{s}", [P, 1]) for s in range(2)]
        n2_h = [sb(f"n2_h{s}", [P, 1]) for s in range(2)]
        k_h = sb("k_h", [P, 1], I32)
        s_h = [sb(f"s_h{s}", [P, 1], I32) for s in range(2)]
        inv_h = [sb(f"inv_h{s}", [P, 1], I32) for s in range(2)]
        sc_y = [sb(f"sc_y{s}", [P, 1]) for s in range(XSLOTS)]
        tw_t = [sb(f"tw_t{s}", [P, 1]) for s in range(XSLOTS)]
        y = [rows[1][:, s, 0:T] for s in range(2)]

        X_BANKS = 6
        ps_x2 = bank[0:X_BANKS]
        ps_xg = [bank[s][:, 0:GROUP * E].rearrange("p (n e) -> p n e", e=E) for s in range(2)]
        ps_lg = [bank[4 + s][:, 0:NT // 2 * E].rearrange("p (n e) -> p n e", e=E) for s in range(2)]
        ps_rank, ps_tot = bank[7][:, 0:E * NT], bank[7][:, E * NT:2 * E * NT]
        ps_list = bank[7][:, 0:2 * QW]
        ps_g, ps_u = bank[0:2], bank[2:4]
        ps_y = bank[4:6]
        ps_n2 = bank[6][:, 0:2]

        consts = sem("consts")
        gw_in = sem("gw_in")
        cond_in = sem("cond_in")
        idx_ready = sem("idx_ready")
        idx_copied = sem("idx_copied")
        zeroed = sem("zeroed")
        pads_out = sem("pads_out")
        xT_ld = [sem(f"xT_ld{s}") for s in range(2)]
        x_ld = [sem(f"x_ld{s}") for s in range(XT_SLOTS)]
        pick_ld = [sem(f"pick_ld{s}") for s in range(PICKS)]
        rows_st = [sem(f"rows_st{s}") for s in range(2)]
        x_st = sem("x_st")
        w_ld = [sem(f"w_ld{e}") for e in range(E)]
        gu_sq = sem("gu_sq")
        w_sq = sem("w_sq")
        n2_ps = sem("n2_ps")
        w_scale = sem("w_scale")
        w_hi = sem("w_hi")
        w_mul = sem("w_mul")
        w_lo = sem("w_lo")
        x_sq = sem("x_sq")
        x_scale = sem("x_scale")
        diag_done = sem("diag_done")
        xg_ps = sem("xg_ps")
        xg_done = sem("xg_done")
        x2_ps = sem("x2_ps")
        x2_hi = sem("x2_hi")
        x2_lo = sem("x2_lo")
        lg_ps = sem("lg_ps")
        lg_done = sem("lg_done")
        gap_done = sem("gap_done")
        gap_exp = sem("gap_exp")
        routed = sem("routed")
        meta_done = sem("meta_done")
        rt = sem("rt")
        ranks_ps = sem("ranks_ps")
        eq_done = sem("eq_done")
        hot_done = sem("hot_done")
        exp_done = sem("exp_done")
        list_ps = sem("list_ps")
        list_done = sem("list_done")
        pool_idx = sem("pool_idx")
        xg_ld = [sem(f"xg_ld{s}") for s in range(XSLOTS)]
        indexed = sem("indexed")
        freed = sem("freed")
        xT_ready = [sem(f"xT_ready{s}") for s in range(2)]
        gu_ps = sem("gu_ps")
        sg_done = sem("sg_done")
        h_done = sem("h_done")
        h_sq = sem("h_sq")
        h_scale = sem("h_scale")
        h_hi = sem("h_hi")
        h_lo = sem("h_lo")
        hT_ready = [sem(f"hT_ready{s}") for s in range(2)]
        pad_zero = sem("pad_zero")
        y_ps = sem("y_ps")
        tw_step = sem("tw_step")
        tw_done = sem("tw_done")
        sc_done = sem("sc_done")
        k_step = sem("k_step")
        inv_done = sem("inv_done")
        scy_done = sem("scy_done")
        y_done = sem("y_done")
        y_st = sem("y_st")

        POOL_CONSTS = 11
        block = ctx.enter_context(nc.Block())

        @block.sync
        def _(sp):
            sp.dma_start(gw_sb[:, :, :], gate_w).then_inc(gw_in, 16)

            def load_xT(g):
                wait(sp, xg_ps, g - 1)
                sp.dma_start(xT_in[g % 2], xT[:, g * GROUP * P:(g + 1) * GROUP * P]
                             .rearrange("(c p) n -> p c n", p=P)).then_inc(xT_ld[g % 2], 16)

            def load_x(g):
                slot, _ = x_slot(g)
                if g >= XT_SLOTS:
                    sp.wait_ge(x2_ps, (g - 1) * GROUP)
                at = X0 + slot * GROUP * T
                sp.dma_start(w_res[:, at:at + GROUP * T].rearrange("p (i t) -> p i t", t=T),
                             x[g * GROUP * P:(g + 1) * GROUP * P, :].rearrange("(i p) t -> p i t", p=P))\
                    .then_inc(x_ld[slot], 16)

            def load_w(e):
                if e == 5:
                    sp.wait_ge(x2_ps, 2 * GROUP)
                stage = w_res[:, (e + 1) * W:(e + 2) * W] if e < E - 1 else w_last
                sp.dma_start(stage, weights[e]).then_inc(w_ld[e], 16)

            def store(g):
                s = g % 2
                sp.wait_ge(x2_hi, (g + 1) * GROUP)
                sp.wait_ge(x2_lo, (g + 1) * GROUP)
                sp.wait_ge(meta_done, g + 1)
                sp.dma_start(x2s[bass.ds(g * GROUP * P, GROUP * P), :]
                             .rearrange("(i p) t -> p i t", p=P), rows[s][:, :, :]).then_inc(rows_st[s], 16)

            def residual(i):
                sp.dma_start(out[i * (N // 4):(i + 1) * (N // 4), :], x[i * (N // 4):(i + 1) * (N // 4), :])\
                    .then_inc(x_st, 16)

            load_xT(0)
            for g in range(1, NG):
                load_xT(g)
                if g in (1, 2, 3, 5, 7):
                    load_w(g - 1 - g // 5 - g // 7)
            load_x(0)
            load_x(1)
            load_x(2)
            load_x(3)
            residual(0)
            residual(1)
            store(0)
            load_w(5)
            store(1)
            for g in range(2, 6):
                load_x(g + 2)
                store(g)
            sp.wait_ge(x2_ps, NT)
            load_w(6)
            load_w(7)
            store(6)
            store(7)
            residual(2)
            sp.wait_ge(zeroed, 1)
            sp.dma_start(x2s[N:N + P, :], zero_row).then_inc(pads_out, 16)
            sp.dma_start(out[N:N + P, :], zero_row[:, 0:T]).then_inc(pads_out, 16)
            sp.wait_ge(xg_ld[XSLOTS - 1], 16)
            residual(3)

        @block.gpsimd
        def _(pool):
            dmas = pool.alloc_register("dmas")
            pool.reg_mov(dmas, 0)

            def stand():
                pool.sem_inc(indexed, 1)

            pool.memset(ident_h[:, :], 0.0).then_inc(zeroed, 1)
            pool.memset(before[:, :], 1.0).then_inc(zeroed, 1)
            pool.memset(ones[:, :], 1.0).then_inc(consts, 1)
            pool.iota(lane[:, :], [[0, 1]], base=0, channel_multiplier=1,
                      allow_small_or_imprecise_dtypes=True).then_inc(consts, 1)
            pool.iota(lane_pad[:, :], [[0, 1]], base=N, channel_multiplier=1,
                      allow_small_or_imprecise_dtypes=True).then_inc(consts, 1)
            pool.iota(rev_e[:, :, :], [[0, NT], [-1, E]], base=E, channel_multiplier=0,
                      allow_small_or_imprecise_dtypes=True).then_inc(consts, 1)
            pool.iota(iota_e[:, :], [[1, E]], base=0, channel_multiplier=0,
                      allow_small_or_imprecise_dtypes=True).then_inc(consts, 1)
            pool.iota(iota_r[:, :], [[1, P]], base=0, channel_multiplier=0,
                      allow_small_or_imprecise_dtypes=True).then_inc(consts, 1)
            pool.iota(iota_q[:, :], [[1, QW]], base=0, channel_multiplier=0,
                      allow_small_or_imprecise_dtypes=True).then_inc(consts, 1)
            pool.iota(iota_j[:, :], [[1, QW]], base=0, channel_multiplier=0,
                      allow_small_or_imprecise_dtypes=True).then_inc(consts, 1)
            pool.iota(tile_m[:, :, :], [[0, TOPK], [1, NT]], base=-NT, channel_multiplier=0,
                      allow_small_or_imprecise_dtypes=True).then_inc(consts, 1)
            pool.wait_ge(zeroed, 3)
            pool.affine_select(out=ident_h[:, :], in_=ident_h[:, :], compare_op=ALU.not_equal, fill=1.0, base=0,
                               pattern=[[-1, P]], channel_multiplier=1).then_inc(consts, 1)
            pool.affine_select(out=before[:, :], in_=before[:, :], compare_op=ALU.is_ge, fill=0.0, base=-1,
                               pattern=[[1, P]], channel_multiplier=-1).then_inc(consts, 1)

            pool.wait_ge(idx_ready, 2)
            def pick(g, s, n):
                wait(pool, pick_ld[s], n * 16 * GROUP)
                wait(pool, diag_done, g - PICKS + 1)
                pool.tensor_copy(pick_idx[s][:, :], cond_i[:, bass.ds(g * GROUP, GROUP)]).then_inc(idx_copied, 1)
                wait(pool, idx_copied, g + 1)
                stand()
                for i in range(GROUP):
                    pool.indirect_dma_start(
                        out=w_pick[s][:, i, :], out_offset=None, in_=cond_w,
                        in_offset=bass.IndirectOffsetOnAxis(ap=pick_idx[s][:, i:i + 1], axis=0),
                    ).then_inc(pick_ld[s], 16)

            for g in range(NG):
                pick(g, g % PICKS, g // PICKS)

            def values(half):
                pool.wait_ge(eq_done, half + 1)
                wait(pool, list_ps, half * 2 * HN)
                for val, ent in ((val_t, ent_t), (val_p, ent_v)):
                    ins = pool.tensor_tensor(val, hot_q, ent[:, half * HN:(half + 1) * HN].unsqueeze(2)
                                             .to_broadcast([P, HN, QW]), ALU.mult)
                ins.then_inc(hot_done, 1)

            muls = [0]

            def low(e, parts):
                for m, (lo, w) in parts:
                    pool.wait_ge(w_hi, 2 * e + m + 1)
                    stage = w_res[:, (e + 1) * W + lo:(e + 1) * W + lo + w]
                    at = e * (2 * W) + lo
                    pool.tensor_tensor(stage, stage, s_w[e % 2][:, m:m + 1].bitcast(F32).to_broadcast([P, w]),
                                       ALU.mult).then_inc(w_mul, 1)
                    muls[0] += 1
                    pool.wait_ge(w_mul, muls[0])
                    pool.tensor_tensor(w_16[:, at + W:at + W + w], stage, w_16[:, at:at + w],
                                       ALU.subtract).then_inc(w_lo, 1)

            low(4, PARTS)
            values(0)
            values(1)
            low(5, PARTS[:1])
            values(2)
            values(3)
            pool.wait_ge(list_done, 1)
            pool.wait_ge(pads_out, 32)
            for s in range(2):
                pool.wait_ge(rows_st[s], 16 * NG // 2)

            def gather(j, u, copies):
                pool.tensor_copy(g_idx[u][:, :], list_i[:, bass.ds(j, 1)]).then_inc(pool_idx, 1)
                pool.wait_ge(pool_idx, copies)
                stand()
                pool.indirect_dma_start(
                    out=xg[u], out_offset=None, in_=x2s[:, :],
                    in_offset=bass.IndirectOffsetOnAxis(ap=g_idx[u][:, :], axis=0)).then_inc(xg_ld[u], 16)

            def scatter(j, s, copies):
                wait(pool, y_st, 16 * j)
                pool.tensor_copy(s_idx[:, :], list_i[:, bass.ds(j, 1)]).then_inc(pool_idx, 1)
                pool.wait_ge(pool_idx, copies)
                pool.wait_ge(y_done, j + 1)
                stand()
                pool.indirect_dma_start(
                    out=out[:, :], out_offset=bass.IndirectOffsetOnAxis(ap=s_idx[:, :], axis=0),
                    in_=y[s], in_offset=None, compute_op=ALU.add).then_inc(y_st, 16)

            def step(j, u, pair):
                pool.wait_ge(xT_ready[u % 2], 16 * (pair + 1))
                pool.wait_ge(sc_done, j + 1)
                pool.wait_ge(tw_done, j + 1)
                gather(j + XSLOTS, u, XSLOTS + 2 * j + (1 if isinstance(j, int) and j == 0 else 0))
                if not (isinstance(j, int) and j == 0):
                    scatter(j - 1, (u - 1) % 2, XSLOTS + 2 * j + 1)

            for u in range(XSLOTS):
                gather(u, u, u + 1)
            pool.wait_ge(x_st, 4 * 16)
            for u in range(XSLOTS):
                step(u, u, u // 2)
            with pool.Fori(1, (TILES - XSLOTS) // XSLOTS) as i:
                for u in range(XSLOTS):
                    step(XSLOTS * i + u, u, 2 * i + u // 2)
            J0 = (TILES - XSLOTS) // XSLOTS * XSLOTS
            for j in range(J0, TILES - XSLOTS):
                step(j, j % XSLOTS, j // 2)
            c = XSLOTS + 2 * (TILES - XSLOTS) - 1
            for j in range(TILES - XSLOTS - 1, TILES):
                c += 1
                scatter(j, j % 2, c)
            pool.wait_ge(y_st, 16 * TILES)

        @block.scalar
        def _(act):
            with nc.allow_non_contiguous_dma(reason="ids of every other batch entry"):
                for b in range(2):
                    act.dma_start(cond_i[b * C:(b + 1) * C, :], cond[b:b + 1, :].to_broadcast([C, NT])).then_inc(cond_in, 16)

            def squares(e, s, n, stage, dump):
                act.wait_ge(w_ld[e], 16)
                wait(act, w_scale, e - 1)
                wait(act, w_sq, e)
                act.activation(dump[:, 0:GU], stage[0], ACT.Square, accum_out=n2_w[s][:, 0:1]).then_inc(gu_sq, 1)
                act.wait_ge(gu_sq, e + 1)
                act.activation(dump[:, 0:DN], stage[1], ACT.Square, accum_out=n2_w[s][:, 1:2]).then_inc(w_sq, 1)

            def exp(half):
                act.wait_ge(gap_done, half + 1)
                part = slice(half * HN, (half + 1) * HN)
                act.activation(gap_e[:, part], gap[:, part], ACT.Exp).then_inc(gap_exp, 1)

            def planes(e, v):
                at = e * (2 * W) + v * W
                return w_16[:, bass.ds(at, GU)], w_16[:, bass.ds(at + GU, DN)]

            def stage_of(e):
                return w_res[:, bass.ds((e + 1) * W, GU)], w_res[:, bass.ds((e + 1) * W + GU, DN)]

            def place_of(e):
                return w_res[:, e * W:e * W + GU // 2].bitcast(BF16)

            def high(e, s, stage):
                act.wait_ge(w_scale, e + 1)
                wait(act, w_lo, 2 * e - 1)
                for m in range(2):
                    act.activation(planes(e, 0)[m], stage[m], ACT.Copy,
                                   scale=s_w[s][:, m:m + 1].bitcast(F32)).then_inc(w_hi, 1)

            for g in range(NG):
                if 2 <= g < 6:
                    squares(g - 2, g % 2, g // 2 - 1, stage_of(g - 2), dump)
                act.wait_ge(xg_ps, g + 1)
                act.activation(xg_sb[:, g * GROUP:(g + 1) * GROUP, :], ps_xg[g % 2], ACT.Copy).then_inc(xg_done, 1)
                if 3 <= g < 7:
                    high(g - 3, (g - 3) % 2, stage_of(g - 3))
                if g == 6:
                    exp(0)
            squares(4, 0, 2, stage_of(4), dump)

            def row_squares(g):
                s = g % 2
                wait(act, x_scale, g)
                wait(act, rows_st[s], g // 2 * 16)
                if g < 2:
                    act.wait_ge(xg_ps, NG)
                for i in range(GROUP):
                    t = g * GROUP + i
                    act.wait_ge(x2_ps, t + 1)
                    act.activation(rows[s][:, i, 0:T], ps_x2[t % X_BANKS][:, :], ACT.Square,
                                   accum_out=n2_x[:, i:i + 1]).then_inc(x_sq, 1)

            def row_high(g):
                act.wait_ge(x_scale, g + 1)
                for i in range(GROUP):
                    act.activation(rows[g % 2][:, i, 0:T // 2].bitcast(F16), ps_x2[(g * GROUP + i) % X_BANKS][:, :],
                                   ACT.Copy, scale=s_x[:, i:i + 1].bitcast(F32)).then_inc(x2_hi, 1)

            for g in range(NG):
                row_squares(g)
                if g == 0:
                    exp(1)
                row_high(g)
                if g == 1:
                    high(4, 0, stage_of(4))
                if g == 3:
                    act.wait_ge(w_lo, 2 * 5)
                    squares(5, 1, 2, stage_of(5), place_of(5))
                if g == 4:
                    high(5, 1, stage_of(5))
            act.wait_ge(w_lo, 2 * (E - 2))
            squares(E - 2, 0, E // 2 - 1, stage_of(E - 2), place_of(E - 2))
            high(E - 2, 0, stage_of(E - 2))
            last = w_last[:, 0:GU], w_last[:, GU:W]
            act.wait_ge(exp_done, 1)
            squares(E - 1, 1, E // 2 - 1, last, dump_last)
            high(E - 1, 1, last)

            def transpose_x(u):
                act.dma_start_transpose(xgT[u % 2].rearrange("p v c n -> p (v c) n"),
                                        xg[u % XSLOTS][:, 0:T].bitcast(F16)).then_inc(xT_ready[u % 2], 16)

            def transpose_h(j, s):
                act.wait_ge(h_hi, j + 1)
                act.wait_ge(h_lo, j + 1)
                wait(act, y_ps, j - 1)
                act.sem_inc(freed, 1)
                act.dma_start_transpose(hT[s].rearrange("p v c n -> p (v c) n"),
                                        h_half[s].rearrange("p v f -> p (v f)")).then_inc(hT_ready[s], 16)

            def hidden(j, u, pair, n_ahead):
                s = u % 2
                wait(act, h_done, j - 1)
                act.wait_ge(sc_done, j + 1)
                act.wait_ge(gu_ps, j + 1)
                act.activation(sg[s], ps_g[s][:, 0:F], ACT.Silu, scale=sc_gu[s][:, 0:1]).then_inc(sg_done, 1)
                if n_ahead is not None:
                    act.wait_ge(xg_ld[(u + 2) % XSLOTS], 16 * (n_ahead + 1))
                    act.sem_inc(freed, 1)
                    transpose_x(u + 2)
                act.wait_ge(h_done, j + 1)
                act.activation(sq, h[s], ACT.Square, accum_out=n2_h[s][:, 0:1]).then_inc(h_sq, 1)
                act.wait_ge(h_scale, j + 1)
                if isinstance(pair, int) and pair == 0:
                    act.wait_ge(pad_zero, 2)
                else:
                    act.wait_ge(hT_ready[s], 16 * pair)
                act.activation(h_half[s][:, 0, 0:F], h[s], ACT.Copy,
                               scale=s_h[s][:, 0:1].bitcast(F32)).then_inc(h_hi, 1)

            def step(j, u, pair, n_ahead):
                hidden(j, u, pair, n_ahead)
                transpose_h(j, u % 2)

            for j in range(2):
                act.wait_ge(xg_ld[j], 16)
                transpose_x(j)
            for j in range(3):
                step(j, j, j // 2, (j + 2) // XSLOTS)
            with act.Fori(0, (TILES - 3) // XSLOTS - 1) as i:
                for u in range(XSLOTS):
                    step(XSLOTS * i + u + 3, u + 3, 2 * i + (u + 3) // 2, i + (u + 5) // XSLOTS)
            for j in range(TILES - XSLOTS, TILES):
                step(j, j, j // 2, (j + 2) // XSLOTS if j + 2 < TILES else None)

        @block.tensor
        def _(pe):
            pe.wait_ge(gw_in, 16)
            def sum_lanes(e):
                pe.wait_ge(w_sq, e + 1)
                wait(pe, w_scale, e)
                pe.matmul(ps_n2, ones_f[:, 0:P], n2_w[e % 2][:, :], start=True, stop=True).then_inc(n2_ps, 1)

            def router(g):
                s = g % 2
                pe.wait_ge(xT_ld[s], (g // 2 + 1) * 16)
                wait(pe, xg_done, g - 1)
                for i in range(GROUP):
                    for c in range(KD):
                        mm = pe.matmul(ps_xg[s][:, i, :], xT_in[s][:, c, i * P:(i + 1) * P], gw_sb[:, c, :],
                                       start=(c == 0), stop=(c == KD - 1))
                mm.then_inc(xg_ps, 1)

            def logits(g):
                pe.wait_ge(xg_done, g + 1)
                pe.wait_ge(diag_done, g + 1)
                half, first_tile = g // (NG // 2), g % (NG // 2) * GROUP
                for i in range(GROUP):
                    t = g * GROUP + i
                    mm = pe.matmul(ps_lg[half][:, first_tile + i, :], arena[:, t * P:(t + 1) * P], xg_sb[:, t, :],
                                   start=True, stop=True)
                mm.then_inc(lg_ps, 1)

            for g in range(NG):
                router(g)
                if 3 <= g < 7:
                    sum_lanes(g - 3)
                if g > 0:
                    logits(g - 1)
            logits(NG - 1)

            def condition(g):
                slot, loads = x_slot(g)
                pe.wait_ge(x_ld[slot], loads * 16)
                for i in range(GROUP):
                    t = g * GROUP + i
                    at = X0 + (slot * GROUP + i) * T
                    wait(pe, x2_hi, t - X_BANKS + 1)
                    wait(pe, x2_lo, t - X_BANKS + 1)
                    pe.matmul(ps_x2[t % X_BANKS][:, :], arena[:, t * P:(t + 1) * P], w_res[:, at:at + T],
                              start=True, stop=True).then_inc(x2_ps, 1)

            pe.wait_ge(xg_done, NG)
            condition(0)
            sum_lanes(4)
            pe.wait_ge(lg_done, 2)
            condition(1)
            pe.wait_ge(routed, 2)
            mem = member[:, :, :].rearrange("p e n -> p (e n)")
            pe.matmul(ps_rank, before[:, :], mem, start=True, stop=True)
            pe.matmul(ps_tot, ones[:, :], mem, start=True, stop=True).then_inc(ranks_ps, 1)

            def list_half(half):
                pe.wait_ge(hot_done, half + 1)
                for t in range(HN):
                    for v, val in enumerate((val_p, val_t)):
                        pe.matmul(ps_list[:, v * QW:(v + 1) * QW], hot_r[:, t, :], val[:, t, :],
                                  start=(half == 0 and t == 0 and v == 0),
                                  stop=(half == 3 and t == HN - 1), skip_group_check=True).then_inc(list_ps, 1)

            for g in range(2, NG):
                condition(g)
                if g == 4:
                    sum_lanes(5)
                if g in (5, 6):
                    list_half(g - 5)
            sum_lanes(E - 2)
            list_half(2)
            sum_lanes(E - 1)
            list_half(3)
            pe.wait_ge(list_done, 1)

            def gate_up(j, s, pair, at):
                pe.wait_ge(xT_ready[s], 16 * (pair + 1))
                wait(pe, h_done, j - 1)
                for c in range(KD):
                    for n, (vx, vw) in enumerate(PRODUCTS):
                        for b, ps in ((0, ps_g), (1, ps_u)):
                            mm = pe.matmul(ps[s][:, 0:F], xgT[s][:, vx, c, :],
                                           w_16[:, bass.ds(at + vw * W + (2 * c + b) * F, F)],
                                           start=(c == 0 and n == 0), stop=(c == KD - 1 and n == len(PRODUCTS) - 1))
                mm.then_inc(gu_ps, 1)

            def down(j, s, pair, at):
                pe.wait_ge(hT_ready[s], 16 * (pair + 1))
                wait(pe, y_done, j - 1)
                for c in range(FC):
                    w = P if c < FC - 1 else FR
                    for n, (vh, vw) in enumerate(PRODUCTS):
                        mm = pe.matmul(ps_y[s][:, :], hT[s][0:w, vh, c, :],
                                       w_16[0:w, bass.ds(at + vw * W + GU + c * T, T)],
                                       start=(c == 0 and n == 0), stop=(c == FC - 1 and n == len(PRODUCTS) - 1))
                mm.then_inc(y_ps, 1)

            def weights_of(j):
                return pe.value_load(exp_i[0:1, bass.ds(j, 1)], min_val=0, max_val=E - 1) * (2 * W)

            pe.wait_ge(w_hi, 2 * E)
            pe.wait_ge(w_lo, 2 * E)
            for j in range(3):
                gate_up(j, j % 2, j // 2, weights_of(j))
                if j == 2:
                    down(0, 0, 0, weights_of(0))
            with pe.Fori(0, (TILES - 3) // XSLOTS) as i:
                for u in range(XSLOTS):
                    j, pair = XSLOTS * i + u + 3, 2 * i + (u + 3) // 2
                    gate_up(j, (u + 3) % 2, pair, weights_of(j))
                    down(j - 2, (u + 1) % 2, pair - 1, weights_of(j - 2))
            for j in range(TILES - 2, TILES):
                down(j, j % 2, j // 2, weights_of(j))

        @block.vector
        def _(dve):
            done = [0]

            def link(ins, base=0):
                done[0] += 1
                ins.then_inc(rt, 1)
                dve.wait_ge(rt, base + done[0])

            link(dve.memset(zero_row, 0.0))
            dve.memset(ones_f[:, :], 1.0).then_inc(zeroed, 1)
            dve.wait_ge(cond_in, 32)
            dve.wait_ge(consts, POOL_CONSTS)
            link(dve.tensor_copy(cond_f[:, :], cond_i[:, :]))
            link(dve.tensor_scalar(idx_lane[:, :], lane[:, :], float(C), -float(C), ALU.is_ge, ALU.mult))
            link(dve.tensor_tensor(idx_lane[:, :], idx_lane[:, :], lane[:, :], ALU.add))
            dve.tensor_scalar(cond_i[:, :], cond_f[:, :], float(C), idx_lane[:, 0:1], ALU.mult,
                              ALU.add).then_inc(idx_ready, 2)

            link(dve.memset(arena[:, 0:NT * P], 0.0))

            def scale(n2_bits, k, s_bits, inv_bits, lk, ready):
                lk(dve.tensor_scalar(k, n2_bits, N2_MIN, MANT, ALU.max, ALU.add))
                lk(dve.tensor_scalar(k, k, 24, None, ALU.logical_shift_right))
                dve.tensor_scalar(s_bits, k, -MANT, S_EXP, ALU.mult, ALU.add).then_inc(ready, 1)
                lk(dve.tensor_scalar(inv_bits, k, MANT, INV_EXP, ALU.mult, ALU.add))

            def scale_w(e, s):
                lk = link
                dve.wait_ge(n2_ps, e + 1)
                wait(dve, w_lo, 2 * (e - 1))
                scale(ps_n2.bitcast(I32), k_w[:, :], s_w[s][:, :], inv_w[:, :, bass.ds(e, 1)].rearrange("p m e -> p (m e)"), lk, w_scale)

            def low(e, s, stage, parts=PARTS):
                for m, (lo, w) in parts:
                    dve.wait_ge(w_hi, 2 * e + m + 1)
                    at = e * (2 * W) + lo
                    dve.scalar_tensor_tensor(out=w_16[:, at + W:at + W + w], in0=stage[m],
                                             scalar=s_w[s][:, m:m + 1].bitcast(F32), in1=w_16[:, at:at + w],
                                             op0=ALU.mult, op1=ALU.subtract).then_inc(w_lo, 1)

            def stage_of(e):
                return w_res[:, bass.ds((e + 1) * W, GU)], w_res[:, bass.ds((e + 1) * W + GU, DN)]

            def diagonal(g, s, n):
                dve.wait_ge(pick_ld[s], (n + 1) * 16 * GROUP)
                for b in range(2):
                    c = slice(b * C, (b + 1) * C)
                    blocks = arena[c, bass.ds(g * GROUP * P, GROUP * P)].rearrange("p (i n) -> p i n", n=P)[:, :, c]
                    copy = dve.tensor_copy(blocks, w_pick[s][c, :, :])
                copy.then_inc(diag_done, 1)

            def spread(a):
                return a.unsqueeze(2).to_broadcast([P, HN, E])

            def top_two(half):
                part = slice(half * HN, (half + 1) * HN)
                dve.wait_ge(lg_ps, (half + 1) * NG // 2)
                link(dve.tensor_copy(lg[:, part, :], ps_lg[half]))
                dve.sem_inc(lg_done, 1)
                src = lg
                for k in range(TOPK):
                    link(dve.tensor_reduce(top[:, k, part], src[:, part, :], AX.X, ALU.max))
                    link(dve.tensor_tensor(eq[:, part, :], src[:, part, :], spread(top[:, k, part]), ALU.is_equal))
                    link(dve.tensor_tensor(cand[:, part, :], eq[:, part, :], rev_e[:, part, :], ALU.mult))
                    link(dve.tensor_reduce(first[:, part], cand[:, part, :], AX.X, ALU.max))
                    link(dve.tensor_tensor(hot[k][:, part, :], rev_e[:, part, :], spread(first[:, part]), ALU.is_equal))
                    if k == 0:
                        link(dve.scalar_tensor_tensor(out=lg2[:, part, :], in0=hot[k][:, part, :], scalar=-BIG,
                                                      in1=lg[:, part, :], op0=ALU.mult, op1=ALU.add))
                        src = lg2
                dve.tensor_tensor(gap[:, part], top[:, 1, part], top[:, 0, part], ALU.subtract).then_inc(gap_done, 1)
                dve.tensor_tensor(member[:, :, part].rearrange("p e n -> p n e"), hot[0][:, part, :], hot[1][:, part, :],
                                  ALU.add).then_inc(routed, 1)

            def softmax(half):
                part = slice(half * HN, (half + 1) * HN)
                dve.wait_ge(gap_exp, half + 1)
                link(dve.tensor_scalar(den[:, part], gap_e[:, part], 1.0, None, ALU.add))
                link(dve.reciprocal(tw[:, 0, part], den[:, part]))
                link(dve.tensor_tensor(tw[:, 1, part], gap_e[:, part], tw[:, 0, part], ALU.mult))
                link(dve.tensor_tensor(eq[:, part, :], hot[0][:, part, :], spread(tw[:, 0, part]), ALU.mult))
                link(dve.tensor_tensor(cand[:, part, :], hot[1][:, part, :], spread(tw[:, 1, part]), ALU.mult))
                link(dve.tensor_tensor(tw_all[:, part, :], eq[:, part, :], cand[:, part, :], ALU.add))

            for g in range(NG // 2):
                diagonal(g, g % PICKS, g // PICKS)
            for e in range(4):
                scale_w(e, e % 2)
                diagonal(4 + e, e % PICKS, 1)
                if e == 3:
                    top_two(0)
                low(e, e % 2, stage_of(e))
            softmax(0)
            dve.wait_ge(xg_ps, NG)
            for s in range(2):
                link(dve.memset(rows[s][:, :, META + E + 1:ROW], 0.0))
            top_two(1)

            def row_scale(g):
                s = g % 2
                dve.wait_ge(x_sq, (g + 1) * GROUP)
                wait(dve, rows_st[s], g // 2 * 16)
                wait(dve, x2_lo, g * GROUP)
                scale(n2_x[:, :].bitcast(I32), k_x[:, :], s_x[:, :], rows[s][:, :, META + E].bitcast(I32), link, x_scale)
                dve.tensor_copy(rows[s][:, :, META:META + E],
                                tw_all[:, g * GROUP:(g + 1) * GROUP, :]).then_inc(meta_done, 1)

            def row_low(g):
                for i in range(GROUP):
                    t = g * GROUP + i
                    dve.wait_ge(x2_hi, t + 1)
                    dve.scalar_tensor_tensor(out=rows[g % 2][:, i, T // 2:T].bitcast(F16), in0=ps_x2[t % X_BANKS][:, :],
                                             scalar=s_x[:, i:i + 1].bitcast(F32),
                                             in1=rows[g % 2][:, i, 0:T // 2].bitcast(F16),
                                             op0=ALU.mult, op1=ALU.subtract).then_inc(x2_lo, 1)

            row_scale(0)
            row_low(0)
            scale_w(4, 0)
            softmax(1)
            row_scale(1)
            row_low(1)

            dve.wait_ge(ranks_ps, 1)
            link(dve.tensor_copy(tot, ps_tot))
            link(dve.tensor_tensor_scan(cum, ones_f[:, :], tot, 0.0, ALU.mult, ALU.add))
            link(dve.tensor_tensor(slots, cum, tot, ALU.subtract))
            link(dve.tensor_tensor(slots, ps_rank, slots, ALU.add))
            ends = cum.rearrange("p (e n) -> p e n", e=E)[:, :, NT - 1]
            link(dve.memset(n_start[:, 0:1], 0.0))
            link(dve.tensor_copy(n_end[:, :], ends))
            link(dve.tensor_copy(n_start[:, 1:E], n_end[:, 0:E - 1]))
            link(dve.tensor_tensor(n_tok[:, :], n_end[:, :], n_start[:, :], ALU.subtract))
            link(dve.tensor_scalar(n_int[:, :], n_tok[:, :], float(P - 1), None, ALU.add))
            link(dve.tensor_scalar(n_int[:, :], n_int[:, :], 7, None, ALU.logical_shift_right))
            link(dve.tensor_copy(n_til[:, :], n_int[:, :]))
            link(dve.tensor_tensor_scan(t_end[:, :], ones_f[:, 0:E], n_til[:, :], 0.0, ALU.mult, ALU.add))
            link(dve.tensor_tensor(off[:, :], t_end[:, :], n_til[:, :], ALU.subtract))
            link(dve.tensor_scalar(off[:, :], off[:, :], float(P), None, ALU.mult))
            link(dve.tensor_tensor(off[:, :], off[:, :], n_start[:, :], ALU.subtract))
            link(dve.tensor_tensor(slots.rearrange("p (e n) -> p e n", e=E),
                                   slots.rearrange("p (e n) -> p e n", e=E),
                                   off[:, :].unsqueeze(2).to_broadcast([P, E, NT]), ALU.add))
            slot_ne = slots.rearrange("p (e n) -> p n e", e=E)
            for k in range(TOPK):
                link(dve.tensor_tensor(prod, hot[k][:, :, :], slot_ne, ALU.mult))
                link(dve.tensor_reduce(entry[:, k * NT:(k + 1) * NT], prod, AX.X, ALU.add))
            link(dve.tensor_copy(entry_i[:, :], entry[:, :]))
            link(dve.tensor_scalar(part_i[:, :], entry_i[:, :], 7, None, ALU.logical_shift_right))
            link(dve.tensor_copy(ent_q[:, :], part_i[:, :]))
            link(dve.tensor_scalar(part_i[:, :], entry_i[:, :], P - 1, None, ALU.bitwise_and))
            link(dve.tensor_copy(ent_r[:, :], part_i[:, :]))
            link(dve.tensor_scalar(ent_v[:, :], ent_r[:, :], -1.0, lane[:, 0:1], ALU.mult, ALU.add))
            link(dve.tensor_copy(ent_t[:, :], tile_m[:, :, :].rearrange("p k n -> p (k n)")))
            def one_hot(half):
                for out_m, iota, ent, w, sem, used in ((hot_q, iota_q, ent_q, QW, hot_done, half),
                                                       (hot_r, iota_r, ent_r, P, list_ps, half * 2 * HN)):
                    wait(dve, sem, used)
                    eq_ins = dve.tensor_tensor(out_m, iota[:, :].unsqueeze(1).to_broadcast([P, HN, w]),
                                               ent[:, half * HN:(half + 1) * HN].unsqueeze(2)
                                               .to_broadcast([P, HN, w]), ALU.is_equal)
                eq_ins.then_inc(eq_done, 1)

            for g in range(2, NG):
                row_scale(g)
                row_low(g)
                if g == 4:
                    scale_w(5, 1)
                if g in (3, 4, 6):
                    one_hot(g - 3 if g < 5 else 2)
                if g == 5:
                    low(5, 1, stage_of(5), PARTS[1:])
            link(dve.tensor_tensor(over, iota_j[:, :].unsqueeze(2).to_broadcast([P, QW, E]),
                                   t_end[:, :].unsqueeze(1).to_broadcast([P, QW, E]), ALU.is_ge))
            link(dve.tensor_reduce(exp_f[:, :], over, AX.X, ALU.add))
            link(dve.tensor_scalar(exp_f[:, :], exp_f[:, :], float(E - 1), None, ALU.min))
            link(dve.tensor_copy(exp_i[:, :], exp_f[:, :]))
            link(dve.tensor_tensor(exp_hot[:, :, :], iota_e[:, :].unsqueeze(1).to_broadcast([P, QW, E]),
                                   exp_f[:, :].unsqueeze(2).to_broadcast([P, QW, E]), ALU.is_equal))
            dve.sem_inc(exp_done, 1)
            scale_w(E - 2, 0)
            one_hot(3)
            low(6, 0, stage_of(6))
            scale_w(E - 1, 1)
            dve.wait_ge(list_ps, 2 * TOPK * NT)
            link(dve.tensor_scalar(list_f[:, :], ps_list[:, 0:QW], lane_pad[:, 0:1], None, ALU.add))
            link(dve.scalar_tensor_tensor(out=list_f[:, :], in0=ps_list[:, QW:2 * QW], scalar=float(P),
                                          in1=list_f[:, :], op0=ALU.mult, op1=ALU.add))
            link(dve.tensor_copy(list_i[:, :], list_f[:, :]))
            dve.sem_inc(list_done, 1)
            for s in range(2):
                dve.memset(h_half[s][:, :, F:FC * P], 0.0).then_inc(pad_zero, 1)
            low(E - 1, 1, (w_last[:, 0:GU], w_last[:, GU:W]))
            for m in range(2):
                link(dve.tensor_tensor(over, exp_hot[:, :, :],
                                       inv_w[:, m, :].bitcast(F32).unsqueeze(1).to_broadcast([P, QW, E]), ALU.mult))
                link(dve.tensor_reduce(inv_t[:, m, :], over, AX.X, ALU.add))

            def weight(j, u, n):
                dve.wait_ge(xg_ld[u], 16 * (n + 1))
                wait(dve, tw_done, j)
                wait(dve, scy_done, j - 3)
                dve.tensor_tensor(tmp_e[:, :], xg[u][:, META:META + E],
                                  exp_hot[:, bass.ds(j, 1), :].rearrange("p a e -> p (a e)"), ALU.mult).then_inc(tw_step, 1)
                wait(dve, h_done, j - 1)
                wait(dve, sg_done, j - 1)
                dve.tensor_tensor(sc_gu[u % 2][:, :], xg[u][:, META + E:META + E + 1],
                                  inv_t[:, 0, bass.ds(j, 1)], ALU.mult).then_inc(sc_done, 1)
                dve.wait_ge(tw_step, j + 1)
                dve.tensor_reduce(tw_t[u][:, :], tmp_e[:, :], AX.X, ALU.add).then_inc(tw_done, 1)

            def hidden(j, u):
                s = u % 2
                dve.wait_ge(sg_done, j + 1)
                dve.wait_ge(sc_done, j + 1)
                wait(dve, h_hi, j - 1)
                wait(dve, h_lo, j - 1)
                dve.scalar_tensor_tensor(out=h[s], in0=ps_u[s][:, 0:F], scalar=sc_gu[s][:, 0:1], in1=sg[s],
                                         op0=ALU.mult, op1=ALU.mult).then_inc(h_done, 1)
                dve.wait_ge(h_sq, j + 1)
                wait(dve, inv_done, j)
                dve.tensor_scalar(k_h[:, :], n2_h[s][:, :].bitcast(I32), N2_MIN, MANT, ALU.max,
                                  ALU.add).then_inc(k_step, 1)
                dve.wait_ge(k_step, 2 * j + 1)
                dve.tensor_scalar(k_h[:, :], k_h[:, :], 24, None, ALU.logical_shift_right).then_inc(k_step, 1)
                dve.wait_ge(k_step, 2 * j + 2)
                dve.tensor_scalar(s_h[s][:, :], k_h[:, :], -MANT, S_EXP, ALU.mult, ALU.add).then_inc(h_scale, 1)
                wait(dve, scy_done, j - 1)
                dve.tensor_scalar(inv_h[s][:, :], k_h[:, :], MANT, INV_EXP, ALU.mult, ALU.add).then_inc(inv_done, 1)
                dve.wait_ge(inv_done, j + 1)
                dve.wait_ge(tw_done, j + 1)
                wait(dve, y_done, j - XSLOTS + 1)
                dve.scalar_tensor_tensor(out=sc_y[u][:, :], in0=inv_h[s][:, :].bitcast(F32), scalar=tw_t[u][:, 0:1],
                                         in1=inv_t[:, 1, bass.ds(j, 1)], op0=ALU.mult, op1=ALU.mult).then_inc(scy_done, 1)
                dve.wait_ge(h_hi, j + 1)
                dve.scalar_tensor_tensor(out=h_half[s][:, 1, 0:F], in0=h[s], scalar=s_h[s][:, 0:1].bitcast(F32),
                                         in1=h_half[s][:, 0, 0:F], op0=ALU.mult, op1=ALU.subtract).then_inc(h_lo, 1)

            def scaled(j, u):
                s = u % 2
                dve.wait_ge(y_ps, j + 1)
                dve.wait_ge(scy_done, j + 1)
                wait(dve, y_st, 16 * (j - 1))
                dve.tensor_scalar(y[s], ps_y[s][:, :], sc_y[u][:, 0:1], None, ALU.mult).then_inc(y_done, 1)

            def step(j, u, n):
                weight(j, u, n)
                hidden(j, u)
                if not (isinstance(j, int) and j < 2):
                    scaled(j - 2, (u - 2) % XSLOTS)

            for j in range(3):
                step(j, j, 0)
            with dve.Fori(0, (TILES - 3) // XSLOTS) as i:
                for u in range(XSLOTS):
                    step(XSLOTS * i + u + 3, (u + 3) % XSLOTS, i + (u + 3) // XSLOTS)
            for j in range(TILES - 2, TILES):
                scaled(j, j % XSLOTS)


def kernel(x, itok_B_1_198, L0_cond_weights, L0_ffn_gate_w, L0_ffn_gate_proj, L0_ffn_up_proj, L0_ffn_down_proj):
    import numpy as np
    import concourse.bacc as bacc
    from concourse.bass_utils import run_bass_kernel_spmd

    B, C, T = x.shape
    E, F, _ = L0_ffn_gate_proj.shape
    N = B * C
    flat = np.ascontiguousarray(x).reshape(N, T)

    def chunked(w):
        return np.transpose(np.asarray(w).reshape(E, F, T // 128, 128), (0, 3, 2, 1))

    gate_up = np.stack([chunked(L0_ffn_gate_proj), chunked(L0_ffn_up_proj)], axis=3).reshape(E, 128, -1)
    FC = -(-F // 128)
    down = np.zeros((E, FC * 128, T), dtype=np.asarray(L0_ffn_down_proj).dtype)
    down[:, 0:F] = np.transpose(np.asarray(L0_ffn_down_proj), (0, 2, 1))
    down = np.transpose(down.reshape(E, FC, 128, T), (0, 2, 1, 3)).reshape(E, 128, -1)

    arrays = {
        "x": flat,
        "xT": np.ascontiguousarray(flat.T),
        "cond": np.ascontiguousarray(np.asarray(itok_B_1_198).reshape(B // 2, 2).T),
        "cond_w": np.ascontiguousarray(L0_cond_weights).reshape(-1, C),
        "gate_w": np.ascontiguousarray(np.transpose(np.asarray(L0_ffn_gate_w).reshape(E, T // 128, 128), (2, 1, 0))),
        "weights": np.concatenate([gate_up, down], axis=2),
    }
    nc = bacc.Bacc("TRN2", target_bir_lowering=False, num_devices=1)
    args = [nc.dram_tensor(name, a.shape, mybir.dt.from_np(a.dtype), kind="ExternalInput").ap()
            for name, a in arrays.items()]
    out = nc.dram_tensor("out", (N + 128, T), F32, kind="ExternalOutput").ap()
    adaln_moe(nc, *args, F, out)
    r = run_bass_kernel_spmd(nc, [arrays], core_ids=[0])
    return r.results[0]["out"][0:N].reshape(B, C, T)
```

```python
from contextlib import ExitStack

import concourse.bass as bass
from concourse import mybir

P = 128
ALU = mybir.AluOpType
ACT = mybir.ActivationFunctionType
AX = mybir.AxisListType
F32 = mybir.dt.float32
BF16 = mybir.dt.bfloat16
F16 = mybir.dt.float16
I32 = mybir.dt.int32

TOPK = 2
GROUP = 4
XSLOTS = 4
BIG = 1.0e30

PRODUCTS = ((0, 0), (0, 1), (1, 0))
MANT = float(1 << 23)
N2_MIN = 67 * MANT
S_EXP = 205 * MANT
INV_EXP = 49 * MANT


def wait(eng, sem, count):
    if not isinstance(count, int) or count > 0:
        eng.wait_ge(sem, count)


def adaln_moe(nc, x, xT, cond, cond_w, gate_w, weights, F, out):
    N, T = x.shape
    C = cond_w.shape[1]
    E, W = weights.shape[0], weights.shape[2]
    KD = T // P
    NT = N // P
    NG = NT // GROUP
    FC = -(-F // P)
    FR = F - (FC - 1) * P
    TILES = TOPK * NT + E - 1
    META = T
    GU, DN = KD * 2 * F, FC * T
    ROW = T + 16
    assert 2 * C == P and KD * P == T and NG == E == 8 and FC == 3 and (TILES - 3) % XSLOTS == 0

    x2s = nc.dram_tensor("x2s", [N + P, ROW], F32, kind="Internal")

    with ExitStack() as ctx:
        def sb(name, shape, dt=F32):
            return ctx.enter_context(nc.sbuf_tensor(name, shape, dt))

        def sem(name):
            return ctx.enter_context(nc.semaphore(name))

        bank = [ctx.enter_context(nc.psum_tensor(f"bank{i}", [P, 512], F32)) for i in range(8)]

        before = sb("before", [P, P], BF16)
        ones = sb("ones", [P, P], BF16)
        ones_f = sb("ones_f", [P, NT * E])
        lane = sb("lane", [P, 1])
        lane_pad = sb("lane_pad", [P, 1])
        rev_e = sb("rev_e", [P, NT, E])
        iota_e = sb("iota_e", [P, E])
        iota_r = sb("iota_r", [P, P], BF16)
        iota_q = sb("iota_q", [P, TILES + 1], BF16)
        iota_j = sb("iota_j", [P, TILES + 1])
        tile_m = sb("tile_m", [P, TOPK, NT])
        idx_lane = sb("idx_lane", [P, 1])
        cond_f = sb("cond_f", [P, NT])
        cond_i = sb("cond_i", [P, NT], I32)
        spare = sb("spare", [P, 2 * FC * P])
        zero_row = spare[:, 0:ROW]
        gw_sb = sb("gw_sb", [P, KD, E])

        w_res = sb("w_res", [P, E * W])
        w_16 = w_res[:, :].bitcast(F16)

        PARTS = tuple(enumerate(((0, GU), (GU, DN))))
        HN = NT // 2
        QW = TILES + 1
        A1 = max(NT * P, W)
        A2 = A1 + (HN * P + 3 * HN * QW) // 2
        A3 = A2 + 4 * NT * E
        arena = sb("arena", [P, max(A3 + 3 * NT * E, A1 + 8 * T)])
        w_last = arena[:, 0:W]

        def stage_of(e):
            place = w_res[:, (e + 1) * W:(e + 2) * W] if e < E - 1 else w_last
            return [place[:, lo:lo + w] for _, (lo, w) in PARTS]


        X_SLOTS = 4
        X0 = E * W - X_SLOTS * GROUP * T

        def x_slot(g):
            return (g, 1) if g < 2 else (2 + g % 2, g // 2)

        PICKS = 4
        w_pick = [arena[:, A1 + s * GROUP * C:A1 + (s + 1) * GROUP * C].rearrange("p (g c) -> p g c", c=C)
                  for s in range(PICKS)]
        dump, dump_last = [arena[:, at:at + GU // 2].bitcast(BF16) for at in (A1 + PICKS * GROUP * C, A2)]
        rows = [sb(f"rows{s}", [P, GROUP, ROW]) for s in range(2)]
        pick_idx = [sb(f"pick_idx{s}", [P, GROUP], I32) for s in range(PICKS)]
        xT_in = [rows[s][:, :, :].rearrange("p g t -> p (g t)")[:, 0:KD * GROUP * P]
                 .rearrange("p (c n) -> p c n", c=KD) for s in range(2)]
        xg_sb = sb("xg_sb", [P, NT, E])
        n2_x = sb("n2_x", [P, GROUP])
        k_x = sb("k_x", [P, GROUP], I32)
        s_x = sb("s_x", [P, GROUP], I32)
        n2_w = [sb(f"n2_w{s}", [P, 2]) for s in range(2)]
        k_w = sb("k_w", [P, 2], I32)
        s_w = [sb(f"s_w{s}", [P, 2], I32) for s in range(2)]
        inv_w = sb("inv_w", [P, 2, E], I32)
        inv_t = sb("inv_t", [P, 2, TILES + 1])
        lg, lg2, eq, cand = [arena[:, A2 + i * NT * E:A2 + (i + 1) * NT * E].rearrange("p (n e) -> p n e", e=E)
                             for i in range(4)]
        top = sb("top", [P, TOPK, NT])
        first = sb("first", [P, NT])
        gap = sb("gap", [P, NT])
        gap_e = sb("gap_e", [P, NT])
        den = sb("den", [P, NT])
        tw = sb("tw", [P, TOPK, NT])
        tw_all = sb("tw_all", [P, NT, E])
        hot = [sb(f"hot{k}", [P, NT, E]) for k in range(TOPK)]
        member = sb("member", [P, E, NT], BF16)

        tot, cum = arena[:, A3:A3 + E * NT], arena[:, A3 + E * NT:A3 + 2 * E * NT]
        slots = tot
        n_end = sb("n_end", [P, E])
        n_start = sb("n_start", [P, E])
        n_tok = sb("n_tok", [P, E])
        n_int = sb("n_int", [P, E], I32)
        n_til = sb("n_til", [P, E])
        t_end = sb("t_end", [P, E])
        off = sb("off", [P, E])
        prod = arena[:, A3 + 2 * E * NT:A3 + 3 * E * NT].rearrange("p (n e) -> p n e", e=E)
        entry = sb("entry", [P, TOPK * NT])
        entry_i = sb("entry_i", [P, TOPK * NT], I32)
        part_i = sb("part_i", [P, TOPK * NT], I32)
        ent_r = sb("ent_r", [P, TOPK * NT], BF16)
        ent_q = sb("ent_q", [P, TOPK * NT], BF16)
        ent_v = sb("ent_v", [P, TOPK * NT], BF16)
        ent_t = sb("ent_t", [P, TOPK * NT], BF16)
        one_hots = arena[:, A1:A2].bitcast(BF16)
        hot_r = one_hots[:, 0:HN * P].rearrange("p (n r) -> p n r", r=P)
        hot_q, val_t, val_p = [one_hots[:, HN * P + i * HN * QW:HN * P + (i + 1) * HN * QW]
                               .rearrange("p (n q) -> p n q", q=QW) for i in range(3)]
        list_f = sb("list_f", [P, QW])
        list_i = sb("list_i", [P, QW], I32)
        over = arena[:, A2:A2 + QW * E].rearrange("p (q e) -> p q e", e=E)
        exp_f = sb("exp_f", [P, QW])
        exp_i = sb("exp_i", [P, QW], I32)
        exp_hot = sb("exp_hot", [P, QW, E], BF16)

        xg = [rows[0][:, s, :] for s in range(XSLOTS)]
        g_idx = [sb(f"g_idx{s}", [P, 1], I32) for s in range(XSLOTS)]
        s_idx = sb("s_idx", [P, 1], I32)
        xgT = [arena[:, A1 + s * T:A1 + (s + 1) * T].bitcast(F16).rearrange("p (v c n) -> p v c n", v=2, c=KD)
               for s in range(2)]
        sg = [arena[:, A1 + (2 + s) * T:A1 + (2 + s) * T + F] for s in range(2)]
        h = [arena[:, A1 + (4 + s) * T:A1 + (4 + s) * T + F] for s in range(2)]
        sq = arena[:, A1 + 6 * T:A1 + 6 * T + F]
        h_half = [part.bitcast(F16).rearrange("p (v f) -> p v f", v=2)
                  for part in (arena[:, A1 + 7 * T:A1 + 7 * T + FC * P], spare[:, FC * P:2 * FC * P])]
        hT = [part.bitcast(F16).rearrange("p (v c n) -> p v c n", v=2, c=FC)
              for part in (spare[:, 0:FC * P], rows[1][:, 2, 0:FC * P])]
        tmp_e = sb("tmp_e", [P, E])
        sc_gu = [sb(f"sc_gu{s}", [P, 1]) for s in range(2)]
        n2_h = [sb(f"n2_h{s}", [P, 1]) for s in range(2)]
        k_h = sb("k_h", [P, 1], I32)
        s_h = [sb(f"s_h{s}", [P, 1], I32) for s in range(2)]
        inv_h = [sb(f"inv_h{s}", [P, 1], I32) for s in range(2)]
        sc_y = [sb(f"sc_y{s}", [P, 1]) for s in range(XSLOTS)]
        tw_t = [sb(f"tw_t{s}", [P, 1]) for s in range(XSLOTS)]
        y = [rows[1][:, s, 0:T] for s in range(2)]

        X_BANKS = 6
        ps_x2 = bank[0:X_BANKS]
        ps_xg = [bank[s][:, 0:GROUP * E].rearrange("p (n e) -> p n e", e=E) for s in range(2)]
        ps_lg = [bank[4 + s][:, 0:NT // 2 * E].rearrange("p (n e) -> p n e", e=E) for s in range(2)]
        ps_rank, ps_tot = bank[7][:, 0:E * NT], bank[7][:, E * NT:2 * E * NT]
        ps_list = bank[7][:, 0:2 * QW]
        ps_g, ps_u = bank[0:2], bank[2:4]
        ps_y = bank[4:6]
        ps_n2 = bank[6][:, 0:2]

        consts = sem("consts")
        gw_in = sem("gw_in")
        cond_in = sem("cond_in")
        idx_ready = sem("idx_ready")
        idx_copied = sem("idx_copied")
        filled = sem("filled")
        zeroed = sem("zeroed")
        pads_out = sem("pads_out")
        xT_ld = [sem(f"xT_ld{s}") for s in range(2)]
        x_ld = [sem(f"x_ld{s}") for s in range(X_SLOTS)]
        pick_ld = [sem(f"pick_ld{s}") for s in range(PICKS)]
        rows_st = [sem(f"rows_st{s}") for s in range(2)]
        x_st = sem("x_st")
        w_ld = [sem(f"w_ld{e}") for e in range(E)]
        gu_sq = sem("gu_sq")
        w_sq = sem("w_sq")
        n2_ps = sem("n2_ps")
        w_scale = sem("w_scale")
        w_hi = sem("w_hi")
        w_mul = sem("w_mul")
        w_lo = sem("w_lo")
        x_sq = sem("x_sq")
        x_scale = sem("x_scale")
        diag_done = sem("diag_done")
        xg_ps = sem("xg_ps")
        xg_done = sem("xg_done")
        x2_ps = sem("x2_ps")
        x2_hi = sem("x2_hi")
        x2_lo = sem("x2_lo")
        lg_ps = sem("lg_ps")
        lg_done = sem("lg_done")
        gap_done = sem("gap_done")
        gap_exp = sem("gap_exp")
        routed = sem("routed")
        meta_done = sem("meta_done")
        rt = sem("rt")
        ranks_ps = sem("ranks_ps")
        eq_done = sem("eq_done")
        hot_done = sem("hot_done")
        exp_done = sem("exp_done")
        list_ps = sem("list_ps")
        list_done = sem("list_done")
        pool_idx = sem("pool_idx")
        xg_ld = [sem(f"xg_ld{s}") for s in range(XSLOTS)]
        indexed = sem("indexed")
        freed = sem("freed")
        xT_ready = [sem(f"xT_ready{s}") for s in range(2)]
        gu_ps = sem("gu_ps")
        sg_done = sem("sg_done")
        h_done = sem("h_done")
        h_sq = sem("h_sq")
        h_scale = sem("h_scale")
        h_hi = sem("h_hi")
        h_lo = sem("h_lo")
        hT_ready = [sem(f"hT_ready{s}") for s in range(2)]
        pad_zero = sem("pad_zero")
        y_ps = sem("y_ps")
        tw_step = sem("tw_step")
        tw_done = sem("tw_done")
        sc_done = sem("sc_done")
        k_step = sem("k_step")
        inv_done = sem("inv_done")
        scy_done = sem("scy_done")
        y_done = sem("y_done")
        y_st = sem("y_st")

        POOL_CONSTS = 10
        RESIDUALS = 8
        block = ctx.enter_context(nc.Block())

        @block.sync
        def _(sp):
            sp.dma_start(gw_sb[:, :, :], gate_w).then_inc(gw_in, 16)

            def load_xT(g):
                wait(sp, xg_ps, g - 1)
                sp.dma_start(xT_in[g % 2], xT[:, g * GROUP * P:(g + 1) * GROUP * P]
                             .rearrange("(c p) n -> p c n", p=P)).then_inc(xT_ld[g % 2], 16)

            def load_x(g):
                slot, _ = x_slot(g)
                if g >= X_SLOTS:
                    sp.wait_ge(x2_ps, (g - 1) * GROUP)
                at = X0 + slot * GROUP * T
                sp.dma_start(w_res[:, at:at + GROUP * T].rearrange("p (i t) -> p i t", t=T),
                             x[g * GROUP * P:(g + 1) * GROUP * P, :].rearrange("(i p) t -> p i t", p=P))\
                    .then_inc(x_ld[slot], 16)

            def load_w(e):
                stage = w_res[:, (e + 1) * W:(e + 2) * W] if e < E - 1 else w_last
                sp.dma_start(stage, weights[e]).then_inc(w_ld[e], 16)

            def store(g):
                s = g % 2
                sp.wait_ge(x2_hi, (g + 1) * GROUP)
                sp.wait_ge(x2_lo, (g + 1) * GROUP)
                sp.wait_ge(meta_done, g + 1)
                sp.dma_start(x2s[bass.ds(g * GROUP * P, GROUP * P), :]
                             .rearrange("(i p) t -> p i t", p=P), rows[s][:, :, :]).then_inc(rows_st[s], 16)

            def residual(i):
                part = slice(i * (N // RESIDUALS), (i + 1) * (N // RESIDUALS))
                sp.dma_start(out[part, :], x[part, :]).then_inc(x_st, 16)

            EXPERT_AFTER = {1: 0, 2: 1, 3: 2, 5: 3, 7: 4}
            load_xT(0)
            for g in range(1, NG):
                load_xT(g)
                if g in EXPERT_AFTER:
                    load_w(EXPERT_AFTER[g])
            for g in range(X_SLOTS):
                load_x(g)
            for i in range(RESIDUALS // 2):
                residual(i)
            store(0)
            sp.wait_ge(x2_ps, 2 * GROUP)
            load_w(5)
            store(1)
            for g in range(2, 6):
                load_x(g + 2)
                store(g)
            sp.wait_ge(x2_ps, NT)
            load_w(6)
            load_w(7)
            store(6)
            store(7)
            sp.wait_ge(zeroed, 1)
            sp.dma_start(x2s[N:N + P, :], zero_row).then_inc(pads_out, 16)
            sp.dma_start(out[N:N + P, :], zero_row[:, 0:T]).then_inc(pads_out, 16)
            residual(4)
            sp.wait_ge(xg_ld[XSLOTS - 1], 16)
            residual(5)
            for i in range(6, RESIDUALS):
                sp.wait_ge(gu_ps, i - 5)
                residual(i)

        @block.gpsimd
        def _(pool):
            def stand():
                pool.sem_inc(indexed, 1)

            pool.memset(before[:, :], 1.0).then_inc(filled, 1)
            pool.memset(ones[:, :], 1.0).then_inc(consts, 1)
            pool.iota(lane[:, :], [[0, 1]], base=0, channel_multiplier=1,
                      allow_small_or_imprecise_dtypes=True).then_inc(consts, 1)
            pool.iota(lane_pad[:, :], [[0, 1]], base=N, channel_multiplier=1,
                      allow_small_or_imprecise_dtypes=True).then_inc(consts, 1)
            pool.iota(rev_e[:, :, :], [[0, NT], [-1, E]], base=E, channel_multiplier=0,
                      allow_small_or_imprecise_dtypes=True).then_inc(consts, 1)
            pool.iota(iota_e[:, :], [[1, E]], base=0, channel_multiplier=0,
                      allow_small_or_imprecise_dtypes=True).then_inc(consts, 1)
            pool.iota(iota_r[:, :], [[1, P]], base=0, channel_multiplier=0,
                      allow_small_or_imprecise_dtypes=True).then_inc(consts, 1)
            pool.iota(iota_q[:, :], [[1, QW]], base=0, channel_multiplier=0,
                      allow_small_or_imprecise_dtypes=True).then_inc(consts, 1)
            pool.iota(iota_j[:, :], [[1, QW]], base=0, channel_multiplier=0,
                      allow_small_or_imprecise_dtypes=True).then_inc(consts, 1)
            pool.iota(tile_m[:, :, :], [[0, TOPK], [1, NT]], base=-NT, channel_multiplier=0,
                      allow_small_or_imprecise_dtypes=True).then_inc(consts, 1)
            pool.wait_ge(filled, 1)
            pool.affine_select(out=before[:, :], in_=before[:, :], compare_op=ALU.is_ge, fill=0.0, base=-1,
                               pattern=[[1, P]], channel_multiplier=-1).then_inc(consts, 1)

            pool.wait_ge(idx_ready, 2)

            def pick(g):
                s, n = g % PICKS, g // PICKS
                wait(pool, pick_ld[s], n * 16 * GROUP)
                wait(pool, diag_done, g - PICKS + 1)
                pool.tensor_copy(pick_idx[s][:, :], cond_i[:, bass.ds(g * GROUP, GROUP)]).then_inc(idx_copied, 1)
                wait(pool, idx_copied, g + 1)
                stand()
                for i in range(GROUP):
                    pool.indirect_dma_start(
                        out=w_pick[s][:, i, :], out_offset=None, in_=cond_w,
                        in_offset=bass.IndirectOffsetOnAxis(ap=pick_idx[s][:, i:i + 1], axis=0),
                    ).then_inc(pick_ld[s], 16)

            for g in range(NG):
                pick(g)

            def values(half):
                pool.wait_ge(eq_done, half + 1)
                wait(pool, list_ps, half * 2 * HN)
                for val, ent in ((val_t, ent_t), (val_p, ent_v)):
                    ins = pool.tensor_tensor(val, hot_q, ent[:, half * HN:(half + 1) * HN].unsqueeze(2)
                                             .to_broadcast([P, HN, QW]), ALU.mult)
                ins.then_inc(hot_done, 1)

            muls = [0]

            def low(e, parts):
                for m, (lo, w) in parts:
                    pool.wait_ge(w_hi, 2 * e + m + 1)
                    stage = w_res[:, (e + 1) * W + lo:(e + 1) * W + lo + w]
                    at = e * (2 * W) + lo
                    pool.tensor_tensor(stage, stage, s_w[e % 2][:, m:m + 1].bitcast(F32).to_broadcast([P, w]),
                                       ALU.mult).then_inc(w_mul, 1)
                    muls[0] += 1
                    pool.wait_ge(w_mul, muls[0])
                    pool.tensor_tensor(w_16[:, at + W:at + W + w], stage, w_16[:, at:at + w],
                                       ALU.subtract).then_inc(w_lo, 1)

            low(4, PARTS)
            values(0)
            values(1)
            low(5, PARTS[:1])
            values(2)
            values(3)
            pool.wait_ge(list_done, 1)
            pool.wait_ge(pads_out, 32)
            for s in range(2):
                pool.wait_ge(rows_st[s], 16 * NG // 2)

            def gather(j, u, copies):
                pool.tensor_copy(g_idx[u][:, :], list_i[:, bass.ds(j, 1)]).then_inc(pool_idx, 1)
                pool.wait_ge(pool_idx, copies)
                stand()
                pool.indirect_dma_start(
                    out=xg[u], out_offset=None, in_=x2s[:, :],
                    in_offset=bass.IndirectOffsetOnAxis(ap=g_idx[u][:, :], axis=0)).then_inc(xg_ld[u], 16)

            def scatter(j, s, copies):
                wait(pool, y_st, 16 * j)
                pool.tensor_copy(s_idx[:, :], list_i[:, bass.ds(j, 1)]).then_inc(pool_idx, 1)
                pool.wait_ge(pool_idx, copies)
                pool.wait_ge(y_done, j + 1)
                stand()
                pool.indirect_dma_start(
                    out=out[:, :], out_offset=bass.IndirectOffsetOnAxis(ap=s_idx[:, :], axis=0),
                    in_=y[s], in_offset=None, compute_op=ALU.add).then_inc(y_st, 16)

            def refill(j, u, pair, copies):
                pool.wait_ge(xT_ready[u % 2], 16 * (pair + 1))
                pool.wait_ge(sc_done, j + 1)
                pool.wait_ge(tw_done, j + 1)
                gather(j + XSLOTS, u, copies)

            def step(j, u, pair):
                refill(j, u, pair, XSLOTS + 2 * j)
                scatter(j - 1, (u - 1) % 2, XSLOTS + 2 * j + 1)

            for u in range(XSLOTS):
                gather(u, u, u + 1)
            pool.wait_ge(x_st, RESIDUALS * 16)
            refill(0, 0, 0, XSLOTS + 1)
            for u in range(1, XSLOTS):
                step(u, u, u // 2)
            with pool.Fori(1, (TILES - XSLOTS) // XSLOTS) as i:
                for u in range(XSLOTS):
                    step(XSLOTS * i + u, u, 2 * i + u // 2)
            J0 = (TILES - XSLOTS) // XSLOTS * XSLOTS
            for j in range(J0, TILES - XSLOTS):
                step(j, j % XSLOTS, j // 2)
            LEFT = TILES - XSLOTS - 1
            for j in range(LEFT, TILES):
                scatter(j, j % 2, TILES + j + 1)
            pool.wait_ge(y_st, 16 * TILES)

        @block.scalar
        def _(act):
            with nc.allow_non_contiguous_dma(reason="ids of every other batch entry"):
                for b in range(2):
                    act.dma_start(cond_i[b * C:(b + 1) * C, :], cond[b:b + 1, :].to_broadcast([C, NT])).then_inc(cond_in, 16)

            def squares(e, dump):
                s, stage = e % 2, stage_of(e)
                act.wait_ge(w_ld[e], 16)
                wait(act, w_scale, e - 1)
                wait(act, w_sq, e)
                act.activation(dump[:, 0:GU], stage[0], ACT.Square, accum_out=n2_w[s][:, 0:1]).then_inc(gu_sq, 1)
                act.wait_ge(gu_sq, e + 1)
                act.activation(dump[:, 0:DN], stage[1], ACT.Square, accum_out=n2_w[s][:, 1:2]).then_inc(w_sq, 1)

            def exp(half):
                act.wait_ge(gap_done, half + 1)
                part = slice(half * HN, (half + 1) * HN)
                act.activation(gap_e[:, part], gap[:, part], ACT.Exp).then_inc(gap_exp, 1)

            def place_of(e):
                return w_res[:, e * W:e * W + GU // 2].bitcast(BF16)

            def high(e):
                s, stage = e % 2, stage_of(e)
                act.wait_ge(w_scale, e + 1)
                wait(act, w_lo, 2 * e - 1)
                for m, (lo, w) in PARTS:
                    at = e * (2 * W) + lo
                    act.activation(w_16[:, at:at + w], stage[m], ACT.Copy,
                                   scale=s_w[s][:, m:m + 1].bitcast(F32)).then_inc(w_hi, 1)

            for g in range(NG):
                if 2 <= g < 6:
                    squares(g - 2, dump)
                act.wait_ge(xg_ps, g + 1)
                act.activation(xg_sb[:, g * GROUP:(g + 1) * GROUP, :], ps_xg[g % 2], ACT.Copy).then_inc(xg_done, 1)
                if 3 <= g < 7:
                    high(g - 3)
                if g == 6:
                    exp(0)
            squares(4, dump)

            def row_squares(g):
                s = g % 2
                wait(act, x_scale, g)
                wait(act, rows_st[s], g // 2 * 16)
                if g < 2:
                    act.wait_ge(xg_ps, NG)
                for i in range(GROUP):
                    t = g * GROUP + i
                    act.wait_ge(x2_ps, t + 1)
                    act.activation(rows[s][:, i, 0:T], ps_x2[t % X_BANKS][:, :], ACT.Square,
                                   accum_out=n2_x[:, i:i + 1]).then_inc(x_sq, 1)

            def row_high(g):
                act.wait_ge(x_scale, g + 1)
                for i in range(GROUP):
                    act.activation(rows[g % 2][:, i, 0:T // 2].bitcast(F16), ps_x2[(g * GROUP + i) % X_BANKS][:, :],
                                   ACT.Copy, scale=s_x[:, i:i + 1].bitcast(F32)).then_inc(x2_hi, 1)

            for g in range(NG):
                row_squares(g)
                if g == 0:
                    exp(1)
                row_high(g)
                if g == 1:
                    high(4)
                if g == 3:
                    act.wait_ge(w_lo, 2 * 5)
                    squares(5, place_of(5))
                if g == 4:
                    high(5)
            act.wait_ge(w_lo, 2 * (E - 2))
            squares(E - 2, place_of(E - 2))
            high(E - 2)
            act.wait_ge(exp_done, 1)
            squares(E - 1, dump_last)
            high(E - 1)

            def transpose_x(u):
                act.dma_start_transpose(xgT[u % 2].rearrange("p v c n -> p (v c) n"),
                                        xg[u % XSLOTS][:, 0:T].bitcast(F16)).then_inc(xT_ready[u % 2], 16)

            def transpose_h(j, s):
                act.wait_ge(h_hi, j + 1)
                act.wait_ge(h_lo, j + 1)
                wait(act, y_ps, j - 1)
                act.sem_inc(freed, 1)
                act.dma_start_transpose(hT[s].rearrange("p v c n -> p (v c) n"),
                                        h_half[s].rearrange("p v f -> p (v f)")).then_inc(hT_ready[s], 16)

            def hidden(j, u, pair, n_ahead):
                s = u % 2
                wait(act, h_done, j - 1)
                act.wait_ge(sc_done, j + 1)
                act.wait_ge(gu_ps, j + 1)
                act.activation(sg[s], ps_g[s][:, 0:F], ACT.Silu, scale=sc_gu[s][:, 0:1]).then_inc(sg_done, 1)
                if n_ahead is not None:
                    act.wait_ge(xg_ld[(u + 2) % XSLOTS], 16 * (n_ahead + 1))
                    act.sem_inc(freed, 1)
                    transpose_x(u + 2)
                act.wait_ge(h_done, j + 1)
                act.activation(sq, h[s], ACT.Square, accum_out=n2_h[s][:, 0:1]).then_inc(h_sq, 1)
                act.wait_ge(h_scale, j + 1)
                wait(act, hT_ready[s], 16 * pair)
                act.activation(h_half[s][:, 0, 0:F], h[s], ACT.Copy,
                               scale=s_h[s][:, 0:1].bitcast(F32)).then_inc(h_hi, 1)

            def step(j, u, pair, n_ahead):
                hidden(j, u, pair, n_ahead)
                transpose_h(j, u % 2)

            act.wait_ge(pad_zero, 2)
            for j in range(2):
                act.wait_ge(xg_ld[j], 16)
                transpose_x(j)
            for j in range(3):
                step(j, j, j // 2, (j + 2) // XSLOTS)
            with act.Fori(0, (TILES - 3) // XSLOTS - 1) as i:
                for u in range(XSLOTS):
                    step(XSLOTS * i + u + 3, u + 3, 2 * i + (u + 3) // 2, i + (u + 5) // XSLOTS)
            for j in range(TILES - XSLOTS, TILES):
                step(j, j, j // 2, (j + 2) // XSLOTS if j + 2 < TILES else None)

        @block.tensor
        def _(pe):
            pe.wait_ge(gw_in, 16)

            def sum_lanes(e):
                pe.wait_ge(w_sq, e + 1)
                wait(pe, w_scale, e)
                pe.matmul(ps_n2, ones_f[:, 0:P], n2_w[e % 2][:, :], start=True, stop=True).then_inc(n2_ps, 1)

            def router(g):
                s = g % 2
                pe.wait_ge(xT_ld[s], (g // 2 + 1) * 16)
                wait(pe, xg_done, g - 1)
                for i in range(GROUP):
                    for c in range(KD):
                        mm = pe.matmul(ps_xg[s][:, i, :], xT_in[s][:, c, i * P:(i + 1) * P], gw_sb[:, c, :],
                                       start=(c == 0), stop=(c == KD - 1))
                mm.then_inc(xg_ps, 1)

            def logits(g):
                pe.wait_ge(xg_done, g + 1)
                pe.wait_ge(diag_done, g + 1)
                half, first_tile = g // (NG // 2), g % (NG // 2) * GROUP
                for i in range(GROUP):
                    t = g * GROUP + i
                    mm = pe.matmul(ps_lg[half][:, first_tile + i, :], arena[:, t * P:(t + 1) * P], xg_sb[:, t, :],
                                   start=True, stop=True)
                mm.then_inc(lg_ps, 1)

            for g in range(NG):
                router(g)
                if 3 <= g < 7:
                    sum_lanes(g - 3)
                if g > 0:
                    logits(g - 1)
            logits(NG - 1)

            def condition(g):
                slot, loads = x_slot(g)
                pe.wait_ge(x_ld[slot], loads * 16)
                for i in range(GROUP):
                    t = g * GROUP + i
                    at = X0 + (slot * GROUP + i) * T
                    wait(pe, x2_hi, t - X_BANKS + 1)
                    wait(pe, x2_lo, t - X_BANKS + 1)
                    pe.matmul(ps_x2[t % X_BANKS][:, :], arena[:, t * P:(t + 1) * P], w_res[:, at:at + T],
                              start=True, stop=True).then_inc(x2_ps, 1)

            pe.wait_ge(xg_done, NG)
            condition(0)
            sum_lanes(4)
            pe.wait_ge(lg_done, 2)
            condition(1)
            pe.wait_ge(routed, 2)
            mem = member[:, :, :].rearrange("p e n -> p (e n)")
            pe.matmul(ps_rank, before[:, :], mem, start=True, stop=True)
            pe.matmul(ps_tot, ones[:, :], mem, start=True, stop=True).then_inc(ranks_ps, 1)

            def list_half(half):
                pe.wait_ge(hot_done, half + 1)
                for t in range(HN):
                    for v, val in enumerate((val_p, val_t)):
                        pe.matmul(ps_list[:, v * QW:(v + 1) * QW], hot_r[:, t, :], val[:, t, :],
                                  start=(half == 0 and t == 0 and v == 0),
                                  stop=(half == 3 and t == HN - 1), skip_group_check=True).then_inc(list_ps, 1)

            LISTS_AFTER = {5: 0, 6: 1}
            for g in range(2, NG):
                condition(g)
                if g == 4:
                    sum_lanes(5)
                if g in LISTS_AFTER:
                    list_half(LISTS_AFTER[g])
            sum_lanes(E - 2)
            list_half(2)
            sum_lanes(E - 1)
            list_half(3)
            pe.wait_ge(list_done, 1)

            def gate_up(j, s, pair, at):
                pe.wait_ge(xT_ready[s], 16 * (pair + 1))
                wait(pe, h_done, j - 1)
                for c in range(KD):
                    for n, (vx, vw) in enumerate(PRODUCTS):
                        for b, ps in ((0, ps_g), (1, ps_u)):
                            mm = pe.matmul(ps[s][:, 0:F], xgT[s][:, vx, c, :],
                                           w_16[:, bass.ds(at + vw * W + (2 * c + b) * F, F)],
                                           start=(c == 0 and n == 0), stop=(c == KD - 1 and n == len(PRODUCTS) - 1))
                mm.then_inc(gu_ps, 1)

            def down(j, s, pair, at):
                pe.wait_ge(hT_ready[s], 16 * (pair + 1))
                wait(pe, y_done, j - 1)
                for c in range(FC):
                    w = P if c < FC - 1 else FR
                    for n, (vh, vw) in enumerate(PRODUCTS):
                        mm = pe.matmul(ps_y[s][:, :], hT[s][0:w, vh, c, :],
                                       w_16[0:w, bass.ds(at + vw * W + GU + c * T, T)],
                                       start=(c == 0 and n == 0), stop=(c == FC - 1 and n == len(PRODUCTS) - 1))
                mm.then_inc(y_ps, 1)

            def weights_of(j):
                return pe.value_load(exp_i[0:1, bass.ds(j, 1)], min_val=0, max_val=E - 1) * (2 * W)

            pe.wait_ge(w_hi, 2 * E)
            pe.wait_ge(w_lo, 2 * E)
            for j in range(3 + XSLOTS):
                gate_up(j, j % 2, j // 2, weights_of(j))
                if j >= 2:
                    down(j - 2, j % 2, j // 2 - 1, weights_of(j - 2))
            with pe.Fori(1, (TILES - 3) // XSLOTS) as i:
                for u in range(XSLOTS):
                    j, pair = XSLOTS * i + u + 3, 2 * i + (u + 3) // 2
                    gate_up(j, (u + 3) % 2, pair, weights_of(j))
                    down(j - 2, (u + 1) % 2, pair - 1, weights_of(j - 2))
            for j in range(TILES - 2, TILES):
                down(j, j % 2, j // 2, weights_of(j))

        @block.vector
        def _(dve):
            done = [0]

            def link(ins):
                done[0] += 1
                ins.then_inc(rt, 1)
                dve.wait_ge(rt, done[0])

            dve.memset(zero_row, 0.0).then_inc(zeroed, 1)
            link(dve.memset(ones_f[:, :], 1.0))
            dve.wait_ge(cond_in, 32)
            dve.wait_ge(consts, POOL_CONSTS)
            link(dve.tensor_copy(cond_f[:, :], cond_i[:, :]))
            link(dve.tensor_scalar(idx_lane[:, :], lane[:, :], float(C), -float(C), ALU.is_ge, ALU.mult))
            link(dve.tensor_tensor(idx_lane[:, :], idx_lane[:, :], lane[:, :], ALU.add))
            dve.tensor_scalar(cond_i[:, :], cond_f[:, :], float(C), idx_lane[:, 0:1], ALU.mult,
                              ALU.add).then_inc(idx_ready, 2)

            link(dve.memset(arena[:, 0:NT * P], 0.0))

            def scale(n2_bits, k, s_bits, inv_bits, ready):
                link(dve.tensor_scalar(k, n2_bits, N2_MIN, MANT, ALU.max, ALU.add))
                link(dve.tensor_scalar(k, k, 24, None, ALU.logical_shift_right))
                dve.tensor_scalar(s_bits, k, -MANT, S_EXP, ALU.mult, ALU.add).then_inc(ready, 1)
                link(dve.tensor_scalar(inv_bits, k, MANT, INV_EXP, ALU.mult, ALU.add))

            def scale_w(e):
                dve.wait_ge(n2_ps, e + 1)
                wait(dve, w_lo, 2 * (e - 1))
                scale(ps_n2.bitcast(I32), k_w[:, :], s_w[e % 2][:, :], inv_w[:, :, e], w_scale)

            def low(e, parts=PARTS):
                s, stage = e % 2, stage_of(e)
                for m, (lo, w) in parts:
                    dve.wait_ge(w_hi, 2 * e + m + 1)
                    at = e * (2 * W) + lo
                    dve.scalar_tensor_tensor(out=w_16[:, at + W:at + W + w], in0=stage[m],
                                             scalar=s_w[s][:, m:m + 1].bitcast(F32), in1=w_16[:, at:at + w],
                                             op0=ALU.mult, op1=ALU.subtract).then_inc(w_lo, 1)

            def diagonal(g):
                s, n = g % PICKS, g // PICKS
                dve.wait_ge(pick_ld[s], (n + 1) * 16 * GROUP)
                for b in range(2):
                    c = slice(b * C, (b + 1) * C)
                    blocks = arena[c, bass.ds(g * GROUP * P, GROUP * P)].rearrange("p (i n) -> p i n", n=P)[:, :, c]
                    copy = dve.tensor_copy(blocks, w_pick[s][c, :, :])
                copy.then_inc(diag_done, 1)

            def spread(a):
                return a.unsqueeze(2).to_broadcast([P, HN, E])

            def top_two(half):
                part = slice(half * HN, (half + 1) * HN)
                dve.wait_ge(lg_ps, (half + 1) * NG // 2)
                link(dve.tensor_copy(lg[:, part, :], ps_lg[half]))
                dve.sem_inc(lg_done, 1)
                src = lg
                for k in range(TOPK):
                    link(dve.tensor_reduce(top[:, k, part], src[:, part, :], AX.X, ALU.max))
                    link(dve.tensor_tensor(eq[:, part, :], src[:, part, :], spread(top[:, k, part]), ALU.is_equal))
                    link(dve.tensor_tensor(cand[:, part, :], eq[:, part, :], rev_e[:, part, :], ALU.mult))
                    link(dve.tensor_reduce(first[:, part], cand[:, part, :], AX.X, ALU.max))
                    link(dve.tensor_tensor(hot[k][:, part, :], rev_e[:, part, :], spread(first[:, part]), ALU.is_equal))
                    if k == 0:
                        link(dve.scalar_tensor_tensor(out=lg2[:, part, :], in0=hot[k][:, part, :], scalar=-BIG,
                                                      in1=lg[:, part, :], op0=ALU.mult, op1=ALU.add))
                        src = lg2
                dve.tensor_tensor(gap[:, part], top[:, 1, part], top[:, 0, part], ALU.subtract).then_inc(gap_done, 1)
                dve.tensor_tensor(member[:, :, part].rearrange("p e n -> p n e"), hot[0][:, part, :], hot[1][:, part, :],
                                  ALU.add).then_inc(routed, 1)

            def softmax(half):
                part = slice(half * HN, (half + 1) * HN)
                dve.wait_ge(gap_exp, half + 1)
                link(dve.tensor_scalar(den[:, part], gap_e[:, part], 1.0, None, ALU.add))
                link(dve.reciprocal(tw[:, 0, part], den[:, part]))
                link(dve.tensor_tensor(tw[:, 1, part], gap_e[:, part], tw[:, 0, part], ALU.mult))
                link(dve.tensor_tensor(eq[:, part, :], hot[0][:, part, :], spread(tw[:, 0, part]), ALU.mult))
                link(dve.tensor_tensor(cand[:, part, :], hot[1][:, part, :], spread(tw[:, 1, part]), ALU.mult))
                link(dve.tensor_tensor(tw_all[:, part, :], eq[:, part, :], cand[:, part, :], ALU.add))

            for g in range(NG // 2):
                diagonal(g)
            for e in range(4):
                scale_w(e)
                diagonal(4 + e)
                if e == 3:
                    top_two(0)
                low(e)
            softmax(0)
            dve.wait_ge(xg_ps, NG)
            for s in range(2):
                link(dve.memset(rows[s][:, :, META + E + 1:ROW], 0.0))
            top_two(1)

            def row_scale(g):
                s = g % 2
                dve.wait_ge(x_sq, (g + 1) * GROUP)
                wait(dve, rows_st[s], g // 2 * 16)
                wait(dve, x2_lo, g * GROUP)
                scale(n2_x[:, :].bitcast(I32), k_x[:, :], s_x[:, :], rows[s][:, :, META + E].bitcast(I32), x_scale)
                dve.tensor_copy(rows[s][:, :, META:META + E],
                                tw_all[:, g * GROUP:(g + 1) * GROUP, :]).then_inc(meta_done, 1)

            def row_low(g):
                for i in range(GROUP):
                    t = g * GROUP + i
                    dve.wait_ge(x2_hi, t + 1)
                    dve.scalar_tensor_tensor(out=rows[g % 2][:, i, T // 2:T].bitcast(F16), in0=ps_x2[t % X_BANKS][:, :],
                                             scalar=s_x[:, i:i + 1].bitcast(F32),
                                             in1=rows[g % 2][:, i, 0:T // 2].bitcast(F16),
                                             op0=ALU.mult, op1=ALU.subtract).then_inc(x2_lo, 1)

            row_scale(0)
            row_low(0)
            scale_w(4)
            softmax(1)
            row_scale(1)
            row_low(1)

            dve.wait_ge(ranks_ps, 1)
            link(dve.tensor_copy(tot, ps_tot))
            link(dve.tensor_tensor_scan(cum, ones_f[:, :], tot, 0.0, ALU.mult, ALU.add))
            link(dve.tensor_tensor(slots, cum, tot, ALU.subtract))
            link(dve.tensor_tensor(slots, ps_rank, slots, ALU.add))
            ends = cum.rearrange("p (e n) -> p e n", e=E)[:, :, NT - 1]
            link(dve.memset(n_start[:, 0:1], 0.0))
            link(dve.tensor_copy(n_end[:, :], ends))
            link(dve.tensor_copy(n_start[:, 1:E], n_end[:, 0:E - 1]))
            link(dve.tensor_tensor(n_tok[:, :], n_end[:, :], n_start[:, :], ALU.subtract))
            link(dve.tensor_scalar(n_int[:, :], n_tok[:, :], float(P - 1), None, ALU.add))
            link(dve.tensor_scalar(n_int[:, :], n_int[:, :], 7, None, ALU.logical_shift_right))
            link(dve.tensor_copy(n_til[:, :], n_int[:, :]))
            link(dve.tensor_tensor_scan(t_end[:, :], ones_f[:, 0:E], n_til[:, :], 0.0, ALU.mult, ALU.add))
            link(dve.tensor_tensor(off[:, :], t_end[:, :], n_til[:, :], ALU.subtract))
            link(dve.tensor_scalar(off[:, :], off[:, :], float(P), None, ALU.mult))
            link(dve.tensor_tensor(off[:, :], off[:, :], n_start[:, :], ALU.subtract))
            link(dve.tensor_tensor(slots.rearrange("p (e n) -> p e n", e=E),
                                   slots.rearrange("p (e n) -> p e n", e=E),
                                   off[:, :].unsqueeze(2).to_broadcast([P, E, NT]), ALU.add))
            slot_ne = slots.rearrange("p (e n) -> p n e", e=E)
            for k in range(TOPK):
                link(dve.tensor_tensor(prod, hot[k][:, :, :], slot_ne, ALU.mult))
                link(dve.tensor_reduce(entry[:, k * NT:(k + 1) * NT], prod, AX.X, ALU.add))
            link(dve.tensor_copy(entry_i[:, :], entry[:, :]))
            link(dve.tensor_scalar(part_i[:, :], entry_i[:, :], 7, None, ALU.logical_shift_right))
            link(dve.tensor_copy(ent_q[:, :], part_i[:, :]))
            link(dve.tensor_scalar(part_i[:, :], entry_i[:, :], P - 1, None, ALU.bitwise_and))
            link(dve.tensor_copy(ent_r[:, :], part_i[:, :]))
            link(dve.tensor_scalar(ent_v[:, :], ent_r[:, :], -1.0, lane[:, 0:1], ALU.mult, ALU.add))
            link(dve.tensor_copy(ent_t[:, :], tile_m[:, :, :].rearrange("p k n -> p (k n)")))

            def one_hot(half):
                for out_m, iota, ent, w, sem, used in ((hot_q, iota_q, ent_q, QW, hot_done, half),
                                                       (hot_r, iota_r, ent_r, P, list_ps, half * 2 * HN)):
                    wait(dve, sem, used)
                    eq_ins = dve.tensor_tensor(out_m, iota[:, :].unsqueeze(1).to_broadcast([P, HN, w]),
                                               ent[:, half * HN:(half + 1) * HN].unsqueeze(2)
                                               .to_broadcast([P, HN, w]), ALU.is_equal)
                eq_ins.then_inc(eq_done, 1)

            HOTS_AFTER = {3: 0, 4: 1, 6: 2}
            for g in range(2, NG):
                row_scale(g)
                row_low(g)
                if g == 4:
                    scale_w(5)
                if g in HOTS_AFTER:
                    one_hot(HOTS_AFTER[g])
                if g == 5:
                    low(5, PARTS[1:])
            link(dve.tensor_tensor(over, iota_j[:, :].unsqueeze(2).to_broadcast([P, QW, E]),
                                   t_end[:, :].unsqueeze(1).to_broadcast([P, QW, E]), ALU.is_ge))
            link(dve.tensor_reduce(exp_f[:, :], over, AX.X, ALU.add))
            link(dve.tensor_scalar(exp_f[:, :], exp_f[:, :], float(E - 1), None, ALU.min))
            link(dve.tensor_copy(exp_i[:, :], exp_f[:, :]))
            link(dve.tensor_tensor(exp_hot[:, :, :], iota_e[:, :].unsqueeze(1).to_broadcast([P, QW, E]),
                                   exp_f[:, :].unsqueeze(2).to_broadcast([P, QW, E]), ALU.is_equal))
            dve.sem_inc(exp_done, 1)
            scale_w(E - 2)
            one_hot(3)
            low(E - 2)
            scale_w(E - 1)
            dve.wait_ge(list_ps, 2 * TOPK * NT)
            link(dve.tensor_scalar(list_f[:, :], ps_list[:, 0:QW], lane_pad[:, 0:1], None, ALU.add))
            link(dve.scalar_tensor_tensor(out=list_f[:, :], in0=ps_list[:, QW:2 * QW], scalar=float(P),
                                          in1=list_f[:, :], op0=ALU.mult, op1=ALU.add))
            link(dve.tensor_copy(list_i[:, :], list_f[:, :]))
            dve.sem_inc(list_done, 1)
            for s in range(2):
                dve.memset(h_half[s][:, :, F:FC * P], 0.0).then_inc(pad_zero, 1)
            low(E - 1)
            for m in range(2):
                link(dve.tensor_tensor(over, exp_hot[:, :, :],
                                       inv_w[:, m, :].bitcast(F32).unsqueeze(1).to_broadcast([P, QW, E]), ALU.mult))
                link(dve.tensor_reduce(inv_t[:, m, :], over, AX.X, ALU.add))

            def weight(j, u, n):
                dve.wait_ge(xg_ld[u], 16 * (n + 1))
                wait(dve, tw_done, j)
                wait(dve, scy_done, j - 2)
                dve.tensor_tensor(tmp_e[:, :], xg[u][:, META:META + E],
                                  exp_hot[:, bass.ds(j, 1), :].rearrange("p a e -> p (a e)"), ALU.mult).then_inc(tw_step, 1)
                wait(dve, h_done, j - 1)
                wait(dve, sg_done, j - 1)
                dve.tensor_tensor(sc_gu[u % 2][:, :], xg[u][:, META + E:META + E + 1],
                                  inv_t[:, 0, bass.ds(j, 1)], ALU.mult).then_inc(sc_done, 1)
                dve.wait_ge(tw_step, j + 1)
                dve.tensor_reduce(tw_t[u][:, :], tmp_e[:, :], AX.X, ALU.add).then_inc(tw_done, 1)

            def hidden(j, u):
                s = u % 2
                dve.wait_ge(sg_done, j + 1)
                dve.wait_ge(sc_done, j + 1)
                wait(dve, h_hi, j - 1)
                wait(dve, h_lo, j - 1)
                dve.scalar_tensor_tensor(out=h[s], in0=ps_u[s][:, 0:F], scalar=sc_gu[s][:, 0:1], in1=sg[s],
                                         op0=ALU.mult, op1=ALU.mult).then_inc(h_done, 1)
                dve.wait_ge(h_sq, j + 1)
                wait(dve, inv_done, j)
                dve.tensor_scalar(k_h[:, :], n2_h[s][:, :].bitcast(I32), N2_MIN, MANT, ALU.max,
                                  ALU.add).then_inc(k_step, 1)
                dve.wait_ge(k_step, 2 * j + 1)
                dve.tensor_scalar(k_h[:, :], k_h[:, :], 24, None, ALU.logical_shift_right).then_inc(k_step, 1)
                dve.wait_ge(k_step, 2 * j + 2)
                dve.tensor_scalar(s_h[s][:, :], k_h[:, :], -MANT, S_EXP, ALU.mult, ALU.add).then_inc(h_scale, 1)
                wait(dve, scy_done, j - 1)
                dve.tensor_scalar(inv_h[s][:, :], k_h[:, :], MANT, INV_EXP, ALU.mult, ALU.add).then_inc(inv_done, 1)
                dve.wait_ge(inv_done, j + 1)
                dve.wait_ge(tw_done, j + 1)
                wait(dve, y_done, j - 2)
                dve.scalar_tensor_tensor(out=sc_y[u][:, :], in0=inv_h[s][:, :].bitcast(F32), scalar=tw_t[u][:, 0:1],
                                         in1=inv_t[:, 1, bass.ds(j, 1)], op0=ALU.mult, op1=ALU.mult).then_inc(scy_done, 1)
                dve.wait_ge(h_hi, j + 1)
                dve.scalar_tensor_tensor(out=h_half[s][:, 1, 0:F], in0=h[s], scalar=s_h[s][:, 0:1].bitcast(F32),
                                         in1=h_half[s][:, 0, 0:F], op0=ALU.mult, op1=ALU.subtract).then_inc(h_lo, 1)

            def scaled(j, u):
                s = u % 2
                dve.wait_ge(y_ps, j + 1)
                dve.wait_ge(scy_done, j + 1)
                wait(dve, y_st, 16 * (j - 1))
                dve.tensor_scalar(y[s], ps_y[s][:, :], sc_y[u][:, 0:1], None, ALU.mult).then_inc(y_done, 1)

            def step(j, u, n):
                weight(j, u, n)
                hidden(j, u)
                scaled(j - 2, (u - 2) % XSLOTS)

            for j in range(2):
                weight(j, j, 0)
                hidden(j, j)
            for j in range(2, 3 + XSLOTS):
                step(j, j % XSLOTS, j // XSLOTS)
            with dve.Fori(1, (TILES - 3) // XSLOTS) as i:
                for u in range(XSLOTS):
                    step(XSLOTS * i + u + 3, (u + 3) % XSLOTS, i + (u + 3) // XSLOTS)
            for j in range(TILES - 2, TILES):
                scaled(j, j % XSLOTS)


def kernel(x, itok_B_1_198, L0_cond_weights, L0_ffn_gate_w, L0_ffn_gate_proj, L0_ffn_up_proj, L0_ffn_down_proj):
    import numpy as np
    import concourse.bacc as bacc
    from concourse.bass_utils import run_bass_kernel_spmd

    B, C, T = x.shape
    E, F, _ = L0_ffn_gate_proj.shape
    N = B * C
    flat = np.ascontiguousarray(x).reshape(N, T)

    def chunked(w):
        return np.transpose(np.asarray(w).reshape(E, F, T // 128, 128), (0, 3, 2, 1))

    gate_up = np.stack([chunked(L0_ffn_gate_proj), chunked(L0_ffn_up_proj)], axis=3).reshape(E, 128, -1)
    FC = -(-F // 128)
    down = np.zeros((E, FC * 128, T), dtype=np.asarray(L0_ffn_down_proj).dtype)
    down[:, 0:F] = np.transpose(np.asarray(L0_ffn_down_proj), (0, 2, 1))
    down = np.transpose(down.reshape(E, FC, 128, T), (0, 2, 1, 3)).reshape(E, 128, -1)

    arrays = {
        "x": flat,
        "xT": np.ascontiguousarray(flat.T),
        "cond": np.ascontiguousarray(np.asarray(itok_B_1_198).reshape(B // 2, 2).T),
        "cond_w": np.ascontiguousarray(L0_cond_weights).reshape(-1, C),
        "gate_w": np.ascontiguousarray(np.transpose(np.asarray(L0_ffn_gate_w).reshape(E, T // 128, 128), (2, 1, 0))),
        "weights": np.concatenate([gate_up, down], axis=2),
    }
    nc = bacc.Bacc("TRN2", target_bir_lowering=False, num_devices=1)
    args = [nc.dram_tensor(name, a.shape, mybir.dt.from_np(a.dtype), kind="ExternalInput").ap()
            for name, a in arrays.items()]
    out = nc.dram_tensor("out", (N + 128, T), F32, kind="ExternalOutput").ap()
    adaln_moe(nc, *args, F, out)
    r = run_bass_kernel_spmd(nc, [arrays], core_ids=[0])
    return r.results[0]["out"][0:N].reshape(B, C, T)
```
